# Optimizing a Trainium2 kernel written in Bass

```python
import numpy as np
import jax
import jax.numpy as jnp

def _softmax(x, axis=-1):
    return jax.nn.softmax(x, axis=axis)

def _gelu(x):
    return jax.nn.gelu(x, approximate=True)

def _silu(x):
    return jax.nn.silu(x)

def _sigmoid(x):
    return jax.nn.sigmoid(x)

def _layernorm(x, axis=-1, eps=1e-05):
    m = jnp.mean(x, axis=axis, keepdims=True)
    v = jnp.var(x, axis=axis, keepdims=True)
    return (x - m) / jnp.sqrt(v + eps)

def _scatter_add(tgt, idx, src, axis=0):
    return tgt.at[idx].add(src)

def _segment_sum(src, seg, n):
    return jax.ops.segment_sum(src, seg, n)
kernel_name = 'mk_conv_preact_d2_conv_nchw64_r2_781dd5'

def setup_inputs(seed: int=0):
    np.random.seed(seed)
    _w = jnp.asarray

    def _rec_inputs():
        import jax
        import jax.numpy as jnp
        _gk = jax.random.key(seed)
        x = -0.000125 + 0.9999 * jax.random.normal(jax.random.fold_in(_gk, 1), (8, 32, 128, 128), jnp.float32)
        return x
    x = _rec_inputs()

    def _L0_conv_setup():
        import jax, jax.numpy as jnp
        import numpy as np
        B, C, O, H, W = (8, 32, 32, 128, 128)
        MX, MY = (16, 16)
        key = jax.random.key(seed)
        ks = jax.random.split(key, 7)
        scale = 1.0 / (C * O)
        return {'x': jax.random.normal(ks[0], (B, C, H, W), dtype=jnp.float32), 'w_x_r': scale * jax.random.normal(ks[1], (C, O, MX), dtype=jnp.float32), 'w_x_i': scale * jax.random.normal(ks[2], (C, O, MX), dtype=jnp.float32), 'w_y_r': scale * jax.random.normal(ks[3], (C, O, MY), dtype=jnp.float32), 'w_y_i': scale * jax.random.normal(ks[4], (C, O, MY), dtype=jnp.float32), 'mix_w': jax.random.normal(ks[5], (O, C), dtype=jnp.float32) * (1.0 / np.sqrt(C)), 'mix_b': jax.random.normal(ks[6], (O,), dtype=jnp.float32) * 0.01}
    _L0_conv_all = _L0_conv_setup()
    _L0_conv_in = {k: v for k, v in _L0_conv_all.items() if k in ('w_x_r', 'w_x_i', 'w_y_r', 'w_y_i', 'mix_w', 'mix_b')}
    del _L0_conv_all

    def _L1_conv_setup():
        import jax, jax.numpy as jnp
        from jax import lax
        import numpy as np
        B, C, O, H, W = (4, 32, 32, 64, 64)
        K, S, P, D = (3, 1, 1, 1)
        K2 = K * K

        def _bilinear_sample(img, ys, xs):
            Hc, Wc = (img.shape[-2], img.shape[-1])
            y0 = jnp.floor(ys)
            x0 = jnp.floor(xs)
            y1 = y0 + 1.0
            x1 = x0 + 1.0
            wy1 = ys - y0
            wy0 = 1.0 - wy1
            wx1 = xs - x0
            wx0 = 1.0 - wx1

            def gather(yi, xi):
                valid = ((yi >= 0) & (yi <= Hc - 1) & (xi >= 0) & (xi <= Wc - 1)).astype(img.dtype)
                yc = jnp.clip(yi, 0, Hc - 1).astype(jnp.int32)
                xc = jnp.clip(xi, 0, Wc - 1).astype(jnp.int32)
                return img[:, yc, xc] * valid[None]
            return gather(y0, x0) * (wy0 * wx0)[None] + gather(y0, x1) * (wy0 * wx1)[None] + gather(y1, x0) * (wy1 * wx0)[None] + gather(y1, x1) * (wy1 * wx1)[None]
        key = jax.random.key(seed)
        k1, k2, k3, k4 = jax.random.split(key, 4)
        x = jax.random.normal(k1, (B, C, H, W), jnp.float32)
        w_om = jax.random.normal(k2, (3 * K2, C, K, K), jnp.float32) * 0.01
        b_om = jax.random.normal(k3, (3 * K2,), jnp.float32) * 0.01
        stdv = 1.0 / float(np.sqrt(C * K * K))
        weight = jax.random.uniform(k4, (O, C, K, K), jnp.float32, -stdv, stdv)
        bias = jnp.zeros((O,), jnp.float32)
        return {'x': x, 'w_om': w_om, 'b_om': b_om, 'weight': weight, 'bias': bias}
    _L1_conv_all = _L1_conv_setup()
    _L1_conv_in = {k: v for k, v in _L1_conv_all.items() if k in ('w_om', 'b_om', 'weight', 'bias')}
    del _L1_conv_all
    return {'x': x, 'L0_conv_w_x_r': _L0_conv_in['w_x_r'], 'L0_conv_w_x_i': _L0_conv_in['w_x_i'], 'L0_conv_w_y_r': _L0_conv_in['w_y_r'], 'L0_conv_w_y_i': _L0_conv_in['w_y_i'], 'L0_conv_mix_w': _L0_conv_in['mix_w'], 'L0_conv_mix_b': _L0_conv_in['mix_b'], 'L1_conv_w_om': _L1_conv_in['w_om'], 'L1_conv_b_om': _L1_conv_in['b_om'], 'L1_conv_weight': _L1_conv_in['weight'], 'L1_conv_bias': _L1_conv_in['bias']}

def reference(x, L0_conv_w_x_r, L0_conv_w_x_i, L0_conv_w_y_r, L0_conv_w_y_i, L0_conv_mix_w, L0_conv_mix_b, L1_conv_w_om, L1_conv_b_om, L1_conv_weight, L1_conv_bias):
    import jax
    import jax.numpy as jnp

    def _L0_conv_ref(x, w_x_r, w_x_i, w_y_r, w_y_i, mix_w, mix_b):
        import jax, jax.numpy as jnp
        import numpy as np
        B, C, O, H, W = (8, 32, 32, 128, 128)
        MX, MY = (16, 16)
        Bs, Cs, Hs, Ws = x.shape
        ft_x = jnp.fft.rfft(x, axis=2, norm='ortho')
        mx = min(MX, Hs // 2 + 1)
        w_x = (w_x_r[:, :, :mx] + 1j * w_x_i[:, :, :mx]).astype(ft_x.dtype)
        box = jnp.einsum('bcx,cox->box', ft_x[:, :, :mx, :].mean(-1), w_x)
        out_x = jnp.zeros_like(ft_x).at[:, :, :mx, :].set(box[..., None])
        x_x = jnp.fft.irfft(out_x, n=Hs, axis=2, norm='ortho')
        ft_y = jnp.fft.rfft(x, axis=3, norm='ortho')
        my = min(MY, Ws // 2 + 1)
        w_y = (w_y_r[:, :, :my] + 1j * w_y_i[:, :, :my]).astype(ft_y.dtype)
        boy = jnp.einsum('bcy,coy->boy', ft_y[:, :, :, :my].mean(2), w_y)
        out_y = jnp.zeros_like(ft_y).at[:, :, :, :my].set(boy[:, :, None, :])
        x_y = jnp.fft.irfft(out_y, n=Ws, axis=3, norm='ortho')
        mix = jnp.einsum('bchw,oc->bohw', x, mix_w) + mix_b[None, :, None, None]
        return x_x + x_y + mix

    def _L1_conv_ref(x, w_om, b_om, weight, bias):
        import jax, jax.numpy as jnp
        from jax import lax
        import numpy as np
        B, C, O, H, W = (4, 32, 32, 64, 64)
        K, S, P, D = (3, 1, 1, 1)
        K2 = K * K

        def _bilinear_sample(img, ys, xs):
            Hc, Wc = (img.shape[-2], img.shape[-1])
            y0 = jnp.floor(ys)
            x0 = jnp.floor(xs)
            y1 = y0 + 1.0
            x1 = x0 + 1.0
            wy1 = ys - y0
            wy0 = 1.0 - wy1
            wx1 = xs - x0
            wx0 = 1.0 - wx1

            def gather(yi, xi):
                valid = ((yi >= 0) & (yi <= Hc - 1) & (xi >= 0) & (xi <= Wc - 1)).astype(img.dtype)
                yc = jnp.clip(yi, 0, Hc - 1).astype(jnp.int32)
                xc = jnp.clip(xi, 0, Wc - 1).astype(jnp.int32)
                return img[:, yc, xc] * valid[None]
            return gather(y0, x0) * (wy0 * wx0)[None] + gather(y0, x1) * (wy0 * wx1)[None] + gather(y1, x0) * (wy1 * wx0)[None] + gather(y1, x1) * (wy1 * wx1)[None]
        om = lax.conv_general_dilated(x, w_om, window_strides=(S, S), padding=[(P, P), (P, P)], rhs_dilation=(D, D), dimension_numbers=('NCHW', 'OIHW', 'NCHW')) + b_om[None, :, None, None]
        Ho, Wo = (om.shape[2], om.shape[3])
        off = om[:, :2 * K2].reshape(-1, K2, 2, Ho, Wo)
        mask = jax.nn.sigmoid(om[:, 2 * K2:])
        dy = off[:, :, 0]
        dx = off[:, :, 1]
        ky, kx = jnp.meshgrid(jnp.arange(K), jnp.arange(K), indexing='ij')
        ky = ky.reshape(-1).astype(x.dtype)
        kx = kx.reshape(-1).astype(x.dtype)
        base_y = (jnp.arange(Ho) * S - P).astype(x.dtype)
        base_x = (jnp.arange(Wo) * S - P).astype(x.dtype)
        ys = dy + (ky * D)[None, :, None, None] + base_y[None, None, :, None]
        xs = dx + (kx * D)[None, :, None, None] + base_x[None, None, None, :]
        vals = jax.vmap(_bilinear_sample)(x, ys, xs)
        vals = vals * mask[:, None]
        Oc = weight.shape[0]
        out = jnp.einsum('bckhw,ock->bohw', vals, weight.reshape(Oc, -1, K2))
        return out + bias[None, :, None, None]

    def _gn(v, G=32, eps=1e-05):
        B_, C_, H_, W_ = v.shape
        g = v.reshape(B_, G, C_ // G, H_, W_)
        m = jnp.mean(g, axis=(2, 3, 4), keepdims=True)
        s = jnp.var(g, axis=(2, 3, 4), keepdims=True)
        return ((g - m) / jnp.sqrt(s + eps)).reshape(v.shape)

    def _ln_c(v, eps=1e-06):
        m = jnp.mean(v, axis=1, keepdims=True)
        s = jnp.var(v, axis=1, keepdims=True)
        return (v - m) / jnp.sqrt(s + eps)

    def _ln_t(v, eps=1e-05):
        m = jnp.mean(v, axis=-1, keepdims=True)
        s = jnp.var(v, axis=-1, keepdims=True)
        return (v - m) / jnp.sqrt(s + eps)

    def _to_tokens(v):
        B_, C_, H_, W_ = v.shape
        return v.reshape(B_, C_, H_ * W_).transpose(0, 2, 1)

    def _from_tokens(t, like):
        B_, C_, H_, W_ = like.shape
        return t.transpose(0, 2, 1).reshape(B_, C_, H_, W_)
    x = x + _L0_conv_ref(_gn(x), L0_conv_w_x_r, L0_conv_w_x_i, L0_conv_w_y_r, L0_conv_w_y_i, L0_conv_mix_w, L0_conv_mix_b)
    x = x + _L1_conv_ref(_gn(x), L1_conv_w_om, L1_conv_b_om, L1_conv_weight, L1_conv_bias)
    return x

_drawn_inputs = setup_inputs


def setup_inputs(seed=0):
    import zlib

    import numpy as np

    out = dict(_drawn_inputs(seed))
    spreads = {'L1_conv_bias': (0.0, 0.1)}
    factors = {'L0_conv_w_x_r': 200.0,
     'L0_conv_w_x_i': 200.0,
     'L0_conv_w_y_r': 200.0,
     'L0_conv_w_y_i': 200.0,
     'L0_conv_mix_b': 6.885,
     'L1_conv_b_om': 25.741}
    for name, (base, spread) in spreads.items():
        noise = np.random.default_rng([zlib.crc32(name.encode()), seed]).standard_normal(out[name].shape)
        drawn = base * np.exp(spread * noise) if base else spread * noise
        out[name] = jnp.asarray(drawn.astype(out[name].dtype))
    for name, factor in factors.items():
        out[name] = (out[name] * factor).astype(out[name].dtype)
    return out
```

```python
import concourse.bass as bass
from concourse import mybir
from contextlib import ExitStack

fp32 = mybir.dt.float32
fp16 = mybir.dt.float16
i32 = mybir.dt.int32
u32 = mybir.dt.uint32
ALU = mybir.AluOpType
ACT = mybir.ActivationFunctionType
AX = mybir.AxisListType

C = 32
H = W = 128
IPG = 4
P = IPG * C
HW = H * W
MODES = 16
KS = 3
TAPS = KS * KS
REACH = 2
NSH = 2 * REACH + 1
REG_R, REG_C = 8, 16
TILE_R, TILE_C = 2, 8
TOP, LEFT = 3, 4
PADR = TOP + H + TOP
PADC = LEFT + W + LEFT
NT = W // TILE_C
NPAIR = H // TILE_R
PX = TILE_R * W
OMC = 3 * TAPS
OMG = IPG * OMC
HYR = 2 * NSH * TAPS
DX0 = 96
STK = DX0 + 2 * TAPS
POSR, ONER = STK, STK + 1
NCH = 2 * TAPS
CH = 2 * PX
VGROUPS = [(0, 1, 2), (3, 4, 5), (6, 7, 8), (9, 10, 11), (12, 13), (14, 15)]
TAPC = TAPS * TILE_R * TILE_C
REP_AT = (5, 8, 11, 14)
XT_AT = (4, 6, 8, 10)
OM_AT = 1
SPLIT_AT, FLAG_AT, OUT_AT = 2, 3, 2
BN_EPS = 1e-5
XCH = 512
NXC = HW // XCH
RPC = XCH // W
LOADS = 4
XHR = 8


def build(nc, g_count, x, wxr, wxi, wyr, wyi, mixt, mixb, womt, bom, wct, biasc,
          dft, inv, ident_d, seldy, selm, sdx, shy, hsconst, cols, gtab, out):
    ctx = ExitStack()
    with ctx:
        def sb(name, shape, dt=fp32):
            return ctx.enter_context(nc.sbuf_tensor(name, shape, dt))

        def pb(name, shape, dt=fp32):
            return ctx.enter_context(nc.psum_tensor(name, shape, dt))

        def sem(name):
            return ctx.enter_context(nc.semaphore(name))

        x1_d = nc.dram_tensor("x1_scratch", (g_count * P, HW), fp32, kind="Internal").ap()
        xh_d = nc.dram_tensor("xh_scratch", (g_count * P, PADR * PADC), fp32, kind="Internal").ap()
        xt_d = nc.dram_tensor("xt_scratch", (g_count * IPG * HW, C), fp32, kind="Internal").ap()

        AW = TAPS * IPG * PX
        VW = NT * TAPC
        sizes = [AW, AW, VW, VW, NT * P, NT * P, 3 * CH, 3 * CH]
        big = sb("big", [P, max(2 * HW, sum(sizes))])
        areas = [big[:, sum(sizes[:i]):sum(sizes[:i + 1])] for i in range(len(sizes))]
        X = [big[:, g * HW:(g + 1) * HW] for g in range(g_count)]
        A, VS, XT = areas[0:2], areas[2:4], areas[4:6]
        ub, vb = [a.rearrange("p (s n) -> p s n", s=3) for a in areas[6:8]]
        ident = sb("ident", [P, P])
        dft_s = sb("dft_s", [H, 2 * MODES])
        inv_s = sb("inv_s", [2 * MODES, H])
        wsp = sb("wsp", [C, 4, C * MODES])
        mwb = sb("mwb", [P, P])
        mixb_s = sb("mixb_s", [P, 1])
        wom = sb("wom", [P, TAPS, OMG])
        bom_s = sb("bom_s", [OMG, 1])
        wc = sb("wc", [P, TAPS, P])
        bias_s = sb("bias_s", [P, 1])
        seldy_s = sb("seldy_s", [OMG, IPG, STK], fp16)
        selm_s = sb("selm_s", [OMG, IPG, HYR], fp16)
        sdx_s = sb("sdx_s", [P, TAPS, P], fp16)
        shy_s = sb("shy_s", [P, TAPS, TILE_R, P], fp16)
        cols_s = sb("cols_s", [P, 4])
        stats = sb("stats", [P, NXC, 6])
        mv = sb("mv", [P, 2, 2])
        col1 = sb("col1", [P, 2, 8])
        sums = sb("sums", [P, 2, 2, H])
        hats = sb("hats", [P, 2, 2, H])
        rt = sb("rt", [H, 2, 2, P])
        fs = sb("fs", [C, 2, 2, MODES, 3, IPG])
        bx = sb("bx", [C, 2, 2, IPG, 2 * MODES])
        bt = sb("bt", [2 * MODES, 2, 2, P])
        xx = sb("xx", [P, 2, 2, H])
        wm = sb("wm", [P, 2, P])
        wint = sb("wint", [P, PADC, REG_R])
        zero = sb("zero", [P, TOP * PADC])
        win = sb("win", [P, 2, REG_R, PADC])
        stg = win
        x1r = sb("x1r", [P, 2, PX])
        outs = sb("outs", [P, 2, PX])
        om_s = sb("om_s", [OMG, 2, PX])
        om_hi = sb("om_hi", [OMG, 2, PX], fp16)
        om_lo = sb("om_lo", [OMG, 2, PX], fp16)
        reach = sb("reach", [OMG, PX])
        hy_u = sb("hy_u", [HYR, PX])
        hy_v = sb("hy_v", [HYR, PX])
        hy_f = sb("hy_f", [STK, PX])
        hy_h = sb("hy_h", [STK, PX], fp16)
        hs = sb("hs", [P, IPG, 2, PX], fp16)
        flag = sb("flag", [1, 2])
        flag_i = sb("flag_i", [1, 1], i32)
        rmax = sb("rmax", [OMG, 1])

        at = [0]

        def take(rows, n, dt=fp32):
            t = big[0:rows, at[0]:at[0] + n]
            at[0] += n
            return t if dt == fp32 else t.bitcast(dt)

        g_row = take(P, W)
        g_rowT = take(P, P)
        g_tab = take(P, 2 * TAPS + H)
        g_bom = take(P, OMC)
        g_wc = take(KS * C, KS * C).rearrange("p (j o) -> p j o", j=KS)
        g_win = take(C, KS * PADC).rearrange("p (r x) -> p r x", r=KS)
        g_x1 = take(C, W)
        g_om = take(P, OMC)
        g_mask = take(P, TAPS)
        g_pos = take(P, 2 * TAPS)
        g_int = take(P, 2 * TAPS, i32)
        g_flo = take(P, 2 * TAPS)
        g_gt = take(P, 2 * TAPS)
        g_cor = take(P, 4 * TAPS)
        g_cw = take(P, 4 * TAPS)
        g_ok = take(P, 4 * TAPS)
        g_in = take(P, 4 * TAPS)
        g_coef = take(P, 4 * TAPS)
        g_fidx = take(P, 4 * TAPS)
        g_idx = take(P, 4 * TAPS, u32)
        g_val = take(P, 4 * TAPS * C)
        g_tmp = take(P, TAPS * C)
        g_acc = take(P, TAPS * C)
        g_vT = take(KS * C, KS * W)
        g_out = take(C, W)

        pD = [pb(f"pD{i}", [P, 512]) for i in range(2)]
        pH = [pb(f"pH{i}", [P, 512]) for i in range(2)]
        pV = [pb(f"pV{i}", [P, 512]) for i in range(2)]
        pM = pb("pM", [P, 512])
        pR = pb("pR", [P, 512])

        const_ld = sem("const_ld")
        zeroed = sem("zeroed")
        blocks_ld = sem("blocks_ld")
        x_ld = [[sem(f"x_ld{g}_{i}") for i in range(LOADS)] for g in range(g_count)]
        stats_done = sem("stats_done")
        colsum_done = sem("colsum_done")
        colsum_read = sem("colsum_read")
        aggr = sem("aggr")
        sd_done = sem("sd_done")
        dve_own = sem("dve_own")
        hat_done = sem("hat_done")
        hatT_done = sem("hatT_done")
        rt_done = sem("rt_done")
        dft_done = sem("dft_done")
        fs_done = sem("fs_done")
        box_done = sem("box_done")
        bx_done = sem("bx_done")
        boxT_done = sem("boxT_done")
        bt_done = sem("bt_done")
        inv_done = sem("inv_done")
        terms_done = sem("terms_done")
        mix_done = sem("mix_done")
        x1_rows = sem("x1_rows")
        x1_done = sem("x1_done")
        x1_st = sem("x1_st")
        norm1 = sem("norm1")
        xh_done = sem("xh_done")
        xh_st = [sem(f"xh_st{i}") for i in range(2)]
        pad_st = sem("pad_st")
        win_ld = [sem(f"win_ld{i}") for i in range(2)]
        x1_ld = [sem(f"x1_ld{i}") for i in range(2)]
        out_st = [sem(f"out_st{i}") for i in range(2)]
        wint_done = sem("wint_done")
        om_done = sem("om_done")
        om_act = sem("om_act")
        om_hi_done = sem("om_hi_done")
        om_split = sem("om_split")
        flag_done = sem("flag_done")
        rep_done = sem("rep_done")
        hy_abs = sem("hy_abs")
        hy_lin = sem("hy_lin")
        hy_full = sem("hy_full")
        hy_half = sem("hy_half")
        hs_done = sem("hs_done")
        d_done = sem("d_done")
        h_done = sem("h_done")
        abs_done = sem("abs_done")
        lin_done = sem("lin_done")
        a_done = sem("a_done")
        t_done = sem("t_done")
        xt_done = sem("xt_done")
        v_done = sem("v_done")
        v_act = sem("v_act")
        v_dve = sem("v_dve")
        conv_done = sem("conv_done")
        out_ready = sem("out_ready")
        reach_col = sem("reach_col")
        reach_row = sem("reach_row")
        flag_set = sem("flag_set")

        g_const = sem("g_const")
        g_row_ld = sem("g_row_ld")
        g_row_T = sem("g_row_T")
        g_row_copied = sem("g_row_copied")
        g_row_st = sem("g_row_st")
        g_ready = sem("g_ready")
        images = g_count * IPG
        kinds = ("load", "om", "act", "idx", "valT", "copy", "conv", "out", "store", "own")
        g_sem = [{k: sem(f"g_{k}{g}") for k in kinds} for g in range(g_count)]
        g_gather = [[sem(f"g_gather{i}_{m}") for m in range(4)] for i in range(images)]
        OWN = 31

        NCONST = 13
        NBLOCK = 6 * IPG
        N_XH = H // XHR
        LOADROWS = H // LOADS
        LOADCH = NXC // LOADS

        def wait(eng, s, v):
            if not (isinstance(v, int) and v <= 0):
                eng.wait_ge(s, v)

        def steps(eng, step):
            for g in range(g_count):
                def stages(s):
                    return [0 <= s - k < NPAIR for k in range(4)]
                for s in range(4):
                    step(g, s, s % 2, stages(s))
                with eng.Fori(0, (NPAIR - 6) // 2) as j:
                    for q in range(2):
                        step(g, j * 2 + (4 + q), q, [True] * 4)
                for s in range(NPAIR - 2, NPAIR + 3):
                    step(g, s, s % 2, stages(s))

        block = ctx.enter_context(nc.Block())

        @block.sync
        def _(sp):
            for dst, src in ((ident[:, :], ident_d), (dft_s[:, :], dft), (inv_s[:, :], inv),
                             (wsp[:, 0, :], wxr.rearrange("c o f -> c (o f)")),
                             (wsp[:, 1, :], wxi.rearrange("c o f -> c (o f)")),
                             (wsp[:, 2, :], wyr.rearrange("c o f -> c (o f)")),
                             (wsp[:, 3, :], wyi.rearrange("c o f -> c (o f)")),
                             (cols_s[:, :], cols),
                             (seldy_s[:, :, :], seldy), (selm_s[:, :, :], selm),
                             (sdx_s[:, :, :], sdx), (shy_s[:, :, :, :], shy)):
                sp.dma_start(dst, src).then_inc(const_ld, 16)
            for g in range(g_count):
                xg = x[g * IPG:(g + 1) * IPG].rearrange("b c h w -> (b c) (h w)")
                for i in range(LOADS):
                    lo, hi = i * LOADROWS * W, (i + 1) * LOADROWS * W
                    sp.dma_start(X[g][:, lo:hi], xg[:, lo:hi]).then_inc(x_ld[g][i], 16)
            sp.wait_ge(zeroed, 1)
            for b in range(IPG):
                r, m = slice(b * C, (b + 1) * C), slice(b * OMC, (b + 1) * OMC)
                sp.dma_start(mwb[r, r], mixt).then_inc(blocks_ld, 16)
                sp.dma_start(mixb_s[r, :], mixb).then_inc(blocks_ld, 16)
                sp.dma_start(wom[r, :, m], womt.rearrange("k c m -> c k m")).then_inc(blocks_ld, 16)
                sp.dma_start(bom_s[m, :], bom).then_inc(blocks_ld, 16)
                sp.dma_start(wc[r, :, r], wct.rearrange("k c o -> c k o")).then_inc(blocks_ld, 16)
                sp.dma_start(bias_s[r, :], biasc).then_inc(blocks_ld, 16)
            sp.dma_start(hs[POSR:POSR + 2, :, :, :], hsconst).then_inc(const_ld, 16)
            for g in range(g_count):
                for edge in (0, TOP + H):
                    sp.dma_start(xh_d[g * P:(g + 1) * P, edge * PADC:(edge + TOP) * PADC],
                                 zero[:, :]).then_inc(pad_st, 16)
            for g in range(g_count):
                for i in range(LOADS):
                    lo, hi = i * LOADROWS * W, (i + 1) * LOADROWS * W
                    sp.wait_ge(x1_done, g * NXC + (i + 1) * LOADCH)
                    sp.dma_start(x1_d[g * P:(g + 1) * P, lo:hi], X[g][:, lo:hi]).then_inc(x1_st, 16)
            for g in range(g_count):
                with sp.Fori(0, N_XH // 2) as j:
                    for q in range(2):
                        sp.wait_ge(xh_done, j * 2 + (g * N_XH + q + 1))
                        sp.dma_start(xh_d[g * P:(g + 1) * P,
                                          bass.ds(j * (2 * XHR * PADC) + (TOP + q * XHR) * PADC, XHR * PADC)],
                                     stg[:, q, :, :].rearrange("p a b -> p (a b)")).then_inc(xh_st[q], 16)
            sp.wait_ge(pad_st, 16 * 2 * g_count)
            sp.wait_ge(x1_st, 16 * LOADS * g_count)
            for q in range(2):
                sp.wait_ge(xh_st[q], 16 * (N_XH // 2) * g_count)

            def load_window(g, n, q):
                wait(sp, wint_done, n + (g * NPAIR - 1))
                src = n * (TILE_R * PADC)
                sp.dma_start(win[:, q, :, :].rearrange("p a b -> p (a b)"),
                             xh_d[g * P:(g + 1) * P, bass.ds(src, REG_R * PADC)]).then_inc(win_ld[q], 16)

            def step(g, s, q, on):
                if isinstance(s, int) and s == 0:
                    load_window(g, 0, 0)
                if not isinstance(s, int) or s + 1 < NPAIR:
                    load_window(g, s + 1, 1 - q)
                if on[3]:
                    n = s - 3
                    sp.wait_ge(out_ready, n + (g * NPAIR + 1))
                    sp.dma_start(out[g * P:(g + 1) * P, bass.ds(n * PX, PX)], outs[:, 1 - q, :]) \
                        .then_inc(out_st[1 - q], 16)
                if on[1]:
                    n = s - 1
                    wait(sp, out_ready, n + (g * NPAIR - 1))
                    sp.dma_start(x1r[:, 1 - q, :], x1_d[g * P:(g + 1) * P, bass.ds(n * PX, PX)]) \
                        .then_inc(x1_ld[1 - q], 16)
            steps(sp, step)
            for q in range(2):
                sp.wait_ge(out_st[q], 16 * (NPAIR // 2) * g_count)

            sp.wait_ge(flag_set, 1)
            far = sp.value_load(flag_i[0:1, 0:1], min_val=0, max_val=1)
            with sp.If(far > 0):
                sp.dma_start(g_tab, gtab).then_inc(g_const, 16)
                sp.dma_start(g_bom, bom.rearrange("m o -> o m").to_broadcast([P, OMC])).then_inc(g_const, 16)
                sp.dma_start(g_wc, wct.rearrange("(j k) c o -> (k c) j o", j=KS)).then_inc(g_const, 16)
                for g in range(g_count):
                    xt_v = xt_d[g * IPG * HW:(g + 1) * IPG * HW, :].rearrange("(i y x) c -> x y i c", i=IPG, y=H)
                    with sp.Fori(0, H) as r:
                        sp.dma_start(g_row, xh_d[g * P:(g + 1) * P, bass.ds(r * PADC + (TOP * PADC + LEFT), W)]) \
                            .then_inc(g_row_ld, 16)
                        sp.wait_ge(g_row_copied, r + (g * H + 1))
                        sp.nop(nofuse=True)
                        sp.dma_start(xt_v[:, bass.ds(r, 1), :, :].rearrange("x y i c -> x (y i) c"),
                                     g_rowT.rearrange("p (i c) -> p i c", i=IPG)).then_inc(g_row_st, 16)
                        sp.wait_ge(g_row_st, (r + (g * H + 1)) * 16)
                        sp.nop(nofuse=True)
                sp.sem_inc(g_ready, 1)
                for i in range(images):
                    m = g_sem[i // IPG]
                    at0 = (i % IPG) * H
                    with sp.Fori(0, H) as y:
                        sp.dma_start(g_win.rearrange("p r x -> p (r x)"),
                                     xh_d[i * C:(i + 1) * C, bass.ds(y * PADC + (TOP - 1) * PADC, KS * PADC)]) \
                            .then_inc(m["load"], 16)
                        sp.dma_start(g_x1, x1_d[i * C:(i + 1) * C, bass.ds(y * W, W)]).then_inc(m["load"], 16)
                        sp.wait_ge(m["out"], y + (at0 + 1))
                        sp.nop(nofuse=True)
                        sp.dma_start(out[i * C:(i + 1) * C, bass.ds(y * W, W)], g_out).then_inc(m["store"], 16)
                        sp.wait_ge(m["store"], (y + (at0 + 1)) * 16)
                        sp.nop(nofuse=True)

        @block.gpsimd
        def _(pool):
            for t in (mwb[:, :], wom[:, :, :], wc[:, :, :], zero[:, :], stg[:, :, :, :],
                      reach[:, :], hy_f[:, :], hs[:, :, :, :]):
                last = nc.gpsimd.memset(t, 0.0)
            last.then_inc(zeroed, 1)

            def step(g, s, q, on):
                for c in range(NCH):
                    if on[1] and c == 0:
                        n = s + (g * NPAIR - 1)
                        pool.wait_ge(win_ld[1 - q], (n - (1 - q)) * 8 + 16)
                        pool.wait_ge(om_done, n + 1)
                        wait(pool, t_done, n * 4)
                        pool.nop(nofuse=True)
                        nc.gpsimd.tensor_copy(wint[:, :, :].rearrange("p x r -> p r x"),
                                              win[:, 1 - q, :, :]).then_inc(wint_done, 1)
                    if on[1]:
                        ci = (s + (g * NPAIR - 1)) * NCH + c
                        pool.wait_ge(abs_done, ci + 1)
                        wait(pool, a_done, ci - 2)
                        pool.nop(nofuse=True)
                        nc.gpsimd.tensor_scalar(vb[:, c % 3, :], ub[:, c % 3, :], -1.0, 1.0,
                                                ALU.mult, ALU.add).then_inc(lin_done, 1)
                    if on[0]:
                        N = s + g * NPAIR
                        if c == SPLIT_AT:
                            pool.wait_ge(om_act, N + 1)
                            wait(pool, rep_done, N * IPG)
                            pool.nop(nofuse=True)
                            nc.gpsimd.tensor_copy(om_hi[:, :, :], om_s[:, :, :]).then_inc(om_hi_done, 1)
                            pool.wait_ge(om_hi_done, N + 1)
                            nc.gpsimd.tensor_tensor(om_lo[:, :, :], om_s[:, :, :], om_hi[:, :, :],
                                                    ALU.subtract).then_inc(om_split, 1)
                        if c in REP_AT:
                            k = N * IPG + REP_AT.index(c)
                            pool.wait_ge(hy_abs, k + 1)
                            wait(pool, hy_full, k)
                            pool.nop(nofuse=True)
                            nc.gpsimd.tensor_scalar(hy_v[:, :], hy_u[:, :], -1.0, 1.0,
                                                    ALU.mult, ALU.add).then_inc(hy_lin, 1)
            steps(pool, step)

            pool.wait_ge(flag_set, 1)
            far = pool.value_load(flag_i[0:1, 0:1], min_val=0, max_val=1)
            with pool.If(far > 0):
                pool.wait_ge(g_ready, 1)
                for i in range(images):
                    m = g_sem[i // IPG]
                    at0 = (i % IPG) * H
                    with pool.Fori(0, H) as y:
                        pool.wait_ge(m["idx"], y + (at0 + 1))
                        pool.nop(nofuse=True)
                        for k in range(4 * TAPS):
                            nc.gpsimd.indirect_dma_start(
                                out=g_val[:, k * C:(k + 1) * C], out_offset=None, in_=xt_d,
                                in_offset=bass.IndirectOffsetOnAxis(ap=g_idx[:, k:k + 1], axis=0)) \
                                .then_inc(g_gather[i][k // TAPS], 16)
                        pool.wait_ge(m["valT"], y + (at0 + 1))
                        pool.nop(nofuse=True)


        @block.scalar
        def _(act):
            act.wait_ge(const_ld, 16 * NCONST)
            for n in range(2):
                for g in range(g_count):
                    act.wait_ge(aggr, n * g_count + g + 1)
                    nc.scalar.activation(col1[:, g, 5 * n:5 * n + 1], mv[:, g, 1:2], ACT.Sqrt,
                                         bias=cols_s[:, 3:4]).then_inc(sd_done, 1)
            act.wait_ge(zeroed, 1)

            def normalize(g, j, q):
                nc.scalar.activation(
                    stg[:, q, :, LEFT:LEFT + W],
                    X[g][:, bass.ds(j * (2 * XHR * W) + q * XHR * W, XHR * W)]
                    .rearrange("p (a b) -> p a b", b=W),
                    ACT.Identity, bias=col1[:, g, 7:8], scale=col1[:, g, 6:7]).then_inc(xh_done, 1)

            for g in range(g_count):
                act.wait_ge(norm1, g + 1)
                first = 0
                if g == 0:
                    for q in range(2):
                        normalize(g, 0, q)
                    first = 1
                with act.Fori(first, N_XH // 2) as j:
                    for q in range(2):
                        act.wait_ge(xh_st[q], (j + g * (N_XH // 2)) * 16)
                        normalize(g, j, q)
            act.wait_ge(x1_st, 16 * LOADS * g_count)
            act.wait_ge(blocks_ld, 16 * NBLOCK)

            def step(g, s, q, on):
                N = s + g * NPAIR
                for c in range(NCH):
                    if on[1]:
                        ci = (N - 1) * NCH + c
                        act.wait_ge(d_done, ci + 1)
                        wait(act, lin_done, ci - 2)
                        nc.scalar.activation(ub[:, c % 3, :], pD[c % 2][:, :], ACT.Abs).then_inc(abs_done, 1)
                        if c in XT_AT:
                            k = XT_AT.index(c)
                            act.wait_ge(t_done, (N - 1) * 4 + (k + 1))
                            if k == 0:
                                wait(act, v_done, (N - 2) * len(VGROUPS))
                            nc.scalar.activation(XT[1 - q][:, k * 512:(k + 1) * 512], pM[:, :],
                                                 ACT.Copy).then_inc(xt_done, 1)
                    if on[2]:
                        for gi, tiles in enumerate(VGROUPS):
                            if gi % 2 == 0 and tiles[-1] == c:
                                act.wait_ge(v_done, (N - 2) * len(VGROUPS) + (gi + 1))
                                if gi == 0:
                                    wait(act, conv_done, N - 3)
                                lo, hi = tiles[0] * TAPC, (tiles[-1] + 1) * TAPC
                                nc.scalar.activation(VS[q][:, lo:hi], pV[0][:, 0:hi - lo],
                                                     ACT.Copy).then_inc(v_act, 1)
                    if on[0]:
                        if c == OM_AT:
                            act.wait_ge(om_done, N + 1)
                            wait(act, om_split, N)
                            wait(act, flag_done, 2 * N)
                            nc.scalar.activation(om_s[:, 0, :], pM[0:OMG, 0:PX], ACT.Identity,
                                                 bias=bom_s[:, 0:1])
                            nc.scalar.activation(om_s[:, 1, :], pM[0:OMG, 0:PX], ACT.Sigmoid,
                                                 bias=bom_s[:, 0:1]).then_inc(om_act, 1)
                        if c in REP_AT:
                            k = N * IPG + REP_AT.index(c)
                            act.wait_ge(rep_done, k + 1)
                            wait(act, hy_lin, k)
                            wait(act, hs_done, k)
                            nc.scalar.activation(hy_u[:, :], pR[0:HYR, 0:PX], ACT.Abs,
                                                 bias=cols_s[0:HYR, 0:1])
                            nc.scalar.activation(hy_f[DX0:STK, :], pR[DX0:STK, 0:PX],
                                                 ACT.Copy).then_inc(hy_abs, 1)
                        if c - 1 in REP_AT:
                            k = N * IPG + REP_AT.index(c - 1)
                            act.wait_ge(hy_full, k + 1)
                            act.wait_ge(hy_abs, k + 1)
                            nc.scalar.activation(hy_h[:, :], hy_f[:, :], ACT.Copy).then_inc(hy_half, 1)
            steps(act, step)

            act.wait_ge(flag_set, 1)
            far = act.value_load(flag_i[0:1, 0:1], min_val=0, max_val=1)
            with act.If(far > 0):
                for i in range(images):
                    m = g_sem[i // IPG]
                    at0 = (i % IPG) * H
                    with act.Fori(0, H) as y:
                        act.wait_ge(m["own"], y * OWN + (at0 * OWN + 1))
                        nc.scalar.activation(g_mask, g_om[:, 2 * TAPS:OMC], ACT.Sigmoid).then_inc(m["act"], 1)

        @block.vector
        def _(dve):
            own = [0]

            def link(ins):
                own[0] += 1
                ins.then_inc(dve_own, 1)
                dve.wait_ge(dve_own, own[0])

            dve.wait_ge(const_ld, 16 * NCONST)
            dve.wait_ge(zeroed, 1)
            for g in range(g_count):
                for i in range(LOADS):
                    dve.wait_ge(x_ld[g][i], 16)
                    with dve.Fori(i * LOADCH, (i + 1) * LOADCH) as k:
                        part = X[g][:, bass.ds(k * XCH, XCH)]
                        nc.vector.tensor_reduce(sums[:, g, 0, bass.ds(k * RPC, RPC)],
                                                part.rearrange("p (a b) -> p a b", b=W), AX.X, ALU.add)
                        nc.vector.bn_stats(stats[:, bass.ds(k, 1), :].rearrange("p a b -> p (a b)"),
                                           part).then_inc(stats_done, 1)
                dve.wait_ge(stats_done, (g + 1) * NXC)
                nc.vector.bn_aggr(mv[:, g, :], stats[:, :, :].rearrange("p a b -> p (a b)")).then_inc(aggr, 1)
                dve.wait_ge(aggr, g + 1)
            for g in range(g_count):
                dve.wait_ge(colsum_done, g + 1)
                link(nc.vector.tensor_reduce(sums[:, g, 1, :], pD[g][:, :].rearrange("p (r w) -> p w r", w=W),
                                             AX.X, ALU.add))
                dve.wait_ge(sd_done, g + 1)
                link(nc.vector.reciprocal(col1[:, g, 1:2], col1[:, g, 0:1]))
                link(nc.vector.scalar_tensor_tensor(out=col1[:, g, 2:3], in0=mv[:, g, 0:1], scalar=-1.0,
                                                    in1=col1[:, g, 1:2], op0=ALU.mult, op1=ALU.mult))
                link(nc.vector.tensor_scalar(col1[:, g, 3:4], col1[:, g, 1:2], 1.0 / W, None, ALU.mult))
                nc.vector.tensor_scalar(hats[:, g, :, :], sums[:, g, :, :], col1[:, g, 3:4],
                                        col1[:, g, 2:3], ALU.mult, ALU.add).then_inc(hat_done, 1)
                dve.wait_ge(blocks_ld, 16 * NBLOCK)
                nc.vector.scalar_tensor_tensor(out=wm[:, g, :], in0=mwb[:, :], scalar=col1[:, g, 1:2],
                                               in1=ident[:, :], op0=ALU.mult, op1=ALU.add).then_inc(hat_done, 1)
            for g in range(g_count):
                dve.wait_ge(hatT_done, g + 1)
                src = (pM, pR)[g]
                nc.vector.tensor_copy(rt[:, g, :, :].rearrange("p a b -> p (a b)"), src[:, 0:2 * P]) \
                    .then_inc(rt_done, 1)
            for g in range(g_count):
                dve.wait_ge(dft_done, g + 1)
                for d in range(2):
                    f = pH[g][0:C, d * P:(d + 1) * P].rearrange("c (b r f) -> c f b r", b=IPG, r=2)
                    nc.vector.tensor_copy(fs[:, g, d, :, 1, :], f[:, :, :, 0])
                    nc.vector.tensor_copy(fs[:, g, d, :, 2, :], f[:, :, :, 1])
                    last = nc.vector.tensor_scalar(fs[:, g, d, :, 0, :], f[:, :, :, 1], -1.0, None, ALU.mult)
                last.then_inc(fs_done, 1)
            dve.wait_ge(box_done, 1)
            for g in range(g_count):
                for d in range(2):
                    o = (g * 2 + d) * P
                    v = pV[0][0:C, o:o + P].rearrange("c (f r b) -> c b r f", f=MODES, r=2)
                    for b in range(IPG):
                        last = nc.vector.tensor_copy(bx[:, g, d, b, :].rearrange("c (r f) -> c r f", r=2),
                                                     v[:, b])
            last.then_inc(bx_done, 1)
            dve.wait_ge(boxT_done, 1)
            nc.vector.tensor_copy(bt[:, 0:g_count, :, :].rearrange("p a b c -> p (a b c)"),
                                  pV[1][0:2 * MODES, 0:g_count * 2 * P]).then_inc(bt_done, 1)
            dve.wait_ge(inv_done, 1)
            for g in range(g_count):
                link(nc.vector.tensor_tensor(col1[:, g, 4:5], pR[:, g:g + 1], mixb_s[:, :], ALU.add))
                nc.vector.tensor_scalar(xx[:, g, 0, :], pM[:, g * 2 * H:g * 2 * H + H], col1[:, g, 4:5],
                                        None, ALU.add)
                link(nc.vector.tensor_copy(xx[:, g, 1, :], pM[:, g * 2 * H + H:g * 2 * H + 2 * H]))

            for g in range(g_count):
                with dve.Fori(0, NXC // 2) as j:
                    for q in range(2):
                        k = j * 2 + q
                        dve.wait_ge(mix_done, k + (g * NXC + 1))
                        for r in range(RPC):
                            row = j * (2 * RPC) + (q * RPC + r)
                            last = nc.vector.scalar_tensor_tensor(
                                out=X[g][:, bass.ds(j * (2 * XCH) + (q * XCH + r * W), W)],
                                in0=pD[q][:, r * W:(r + 1) * W], scalar=xx[:, g, 0, bass.ds(row, 1)],
                                in1=xx[:, g, 1, :], op0=ALU.add, op1=ALU.add)
                        last.then_inc(x1_rows, 1)
                        dve.wait_ge(x1_rows, k + (g * NXC + 1))
                        nc.vector.bn_stats(stats[:, bass.ds(k, 1), :].rearrange("p a b -> p (a b)"),
                                           X[g][:, bass.ds(j * (2 * XCH) + q * XCH, XCH)]).then_inc(x1_done, 1)
                dve.wait_ge(x1_done, (g + 1) * NXC)
                dve.wait_ge(sd_done, g_count)
                nc.vector.bn_aggr(mv[:, g, :], stats[:, :, :].rearrange("p a b -> p (a b)")).then_inc(aggr, 1)
                dve.wait_ge(aggr, g_count + g + 1)
                dve.wait_ge(sd_done, g_count + g + 1)
                link(nc.vector.reciprocal(col1[:, g, 6:7], col1[:, g, 5:6]))
                nc.vector.scalar_tensor_tensor(out=col1[:, g, 7:8], in0=mv[:, g, 0:1], scalar=-1.0,
                                               in1=col1[:, g, 6:7], op0=ALU.mult, op1=ALU.mult).then_inc(norm1, 1)
            dve.wait_ge(x1_st, 16 * LOADS * g_count)
            dve.wait_ge(xh_done, N_XH * g_count)

            def step(g, s, q, on):
                N = s + g * NPAIR
                for c in range(NCH):
                    bp, k = divmod(c, TAPS)
                    if on[1]:
                        ci = (N - 1) * NCH + c
                        dve.wait_ge(lin_done, ci + 1)
                        dve.wait_ge(h_done, ci + 1)
                        if c == 0:
                            wait(dve, v_done, (N - 2) * len(VGROUPS))
                        o = k * IPG * PX + bp * CH
                        nc.vector.scalar_tensor_tensor(out=A[1 - q][:, o:o + CH], in0=vb[:, c % 3, :],
                                                       scalar=0.0, in1=pH[c % 2][:, :],
                                                       op0=ALU.max, op1=ALU.mult).then_inc(a_done, 1)
                    if on[2]:
                        for gi, tiles in enumerate(VGROUPS):
                            if gi % 2 == 1 and tiles[-1] == c:
                                dve.wait_ge(v_done, (N - 2) * len(VGROUPS) + (gi + 1))
                                if gi == 1:
                                    wait(dve, conv_done, N - 3)
                                lo, hi = tiles[0] * TAPC, (tiles[-1] + 1) * TAPC
                                nc.vector.tensor_copy(VS[q][:, lo:hi], pV[1][:, 0:hi - lo]).then_inc(v_dve, 1)
                    if on[3] and c == OUT_AT:
                        n = N - 3
                        dve.wait_ge(conv_done, n + 1)
                        dve.wait_ge(x1_ld[1 - q], (n - (1 - q)) * 8 + 16)
                        m = (n - (1 - q)) * 8
                        if not (isinstance(m, int) and m == 0):
                            dve.wait_ge(out_st[1 - q], m)
                        nc.vector.scalar_tensor_tensor(out=outs[:, 1 - q, :], in0=pR[:, 0:PX],
                                                       scalar=bias_s[:, 0:1], in1=x1r[:, 1 - q, :],
                                                       op0=ALU.add, op1=ALU.add).then_inc(out_ready, 1)
                    if on[0]:
                        if c == FLAG_AT:
                            dve.wait_ge(om_act, N + 1)
                            for i in range(2):
                                wait(dve, flag_done, 2 * N + i)
                                nc.vector.scalar_tensor_tensor(out=reach[:, :], in0=om_s[:, 0, :],
                                                               scalar=(1.0, -1.0)[i], in1=reach[:, :],
                                                               op0=ALU.mult, op1=ALU.max).then_inc(flag_done, 1)
                        if c in REP_AT:
                            i = N * IPG + REP_AT.index(c)
                            dve.wait_ge(hy_lin, i + 1)
                            wait(dve, hy_half, i)
                            nc.vector.scalar_tensor_tensor(out=hy_f[0:HYR, :], in0=hy_v[:, :], scalar=0.0,
                                                           in1=pR[0:HYR, PX:2 * PX], op0=ALU.max,
                                                           op1=ALU.mult).then_inc(hy_full, 1)
                        if c - 1 in REP_AT:
                            b = REP_AT.index(c - 1)
                            dve.wait_ge(hy_half, N * IPG + b + 1)
                            if b == 0:
                                wait(dve, h_done, (N - 1) * NCH)
                            nc.vector.scalar_tensor_tensor(out=hs[0:STK, b, q, :], in0=hy_h[:, :],
                                                           scalar=cols_s[0:STK, 1:2], in1=hy_f[:, :],
                                                           op0=ALU.mult, op1=ALU.add).then_inc(hs_done, 1)
            steps(dve, step)

            dve.wait_ge(flag_done, 2 * NPAIR * g_count)
            link(nc.vector.tensor_reduce(rmax[:, :], reach[:, :], AX.X, ALU.max))
            nc.vector.tensor_tensor(rmax[:, :], rmax[:, :], cols_s[0:OMG, 2:3], ALU.min).then_inc(reach_col, 1)
            dve.wait_ge(reach_row, 1)
            link(nc.vector.tensor_reduce(flag[:, 0:1], pM[0:1, 0:OMG], AX.X, ALU.max))
            link(nc.vector.tensor_scalar(flag[:, 1:2], flag[:, 0:1], float(REACH), None, ALU.is_gt))
            nc.vector.tensor_copy(flag_i[:, :], flag[:, 1:2]).then_inc(flag_set, 1)
            dve.wait_ge(flag_set, 1)
            far = dve.value_load(flag_i[0:1, 0:1], min_val=0, max_val=1)
            with dve.If(far > 0):
                dve.wait_ge(g_const, 48)
                for g in range(g_count):
                    with dve.Fori(0, H) as r:
                        dve.wait_ge(g_row_T, r + (g * H + 1))
                        nc.vector.tensor_copy(g_rowT, pM[:, 0:P]).then_inc(g_row_copied, 1)

                def v4(t):
                    return t.rearrange("p (a d k) -> p a d k", a=2, d=2)

                for i in range(images):
                    m = g_sem[i // IPG]
                    at0 = (i % IPG) * H
                    with dve.Fori(0, H) as y:
                        done = [0]

                        def chain(ins):
                            done[0] += 1
                            ins.then_inc(m["own"], 1)
                            dve.wait_ge(m["own"], y * OWN + (at0 * OWN + done[0]))

                        v = nc.vector
                        dve.wait_ge(m["om"], y + (at0 + 1))
                        chain(v.tensor_tensor(g_om, pR[:, 0:OMC], g_bom, ALU.add))
                        chain(v.tensor_tensor(g_pos, g_om[:, 0:2 * TAPS], g_tab[:, 0:2 * TAPS], ALU.add))
                        chain(v.tensor_scalar(g_pos[:, 0:TAPS], g_pos[:, 0:TAPS],
                                              g_tab[:, bass.ds(y + 2 * TAPS, 1)], None, ALU.add))
                        chain(v.tensor_scalar(g_pos, g_pos, -2.0, float(H + 1), ALU.max, ALU.min))
                        chain(v.tensor_copy(g_int, g_pos))
                        chain(v.tensor_copy(g_flo, g_int))
                        chain(v.tensor_tensor(g_gt, g_flo, g_pos, ALU.is_gt))
                        chain(v.tensor_tensor(g_cor[:, 0:2 * TAPS], g_flo, g_gt, ALU.subtract))
                        chain(v.tensor_scalar(g_cor[:, 2 * TAPS:], g_cor[:, 0:2 * TAPS], 1.0, None, ALU.add))
                        chain(v.tensor_tensor(g_cw[:, 2 * TAPS:], g_pos, g_cor[:, 0:2 * TAPS], ALU.subtract))
                        chain(v.tensor_scalar(g_cw[:, 0:2 * TAPS], g_cw[:, 2 * TAPS:], -1.0, 1.0,
                                              ALU.mult, ALU.add))
                        chain(v.tensor_scalar(g_ok, g_cor, 0.0, None, ALU.is_ge))
                        chain(v.scalar_tensor_tensor(out=g_in, in0=g_cor, scalar=float(H - 1), in1=g_ok,
                                                     op0=ALU.is_le, op1=ALU.mult))
                        chain(v.tensor_tensor(g_cw, g_cw, g_in, ALU.mult))
                        chain(v.tensor_scalar(g_cor, g_cor, 0.0, float(H - 1), ALU.max, ALU.min))
                        dve.wait_ge(m["act"], y + (at0 + 1))
                        for a in range(2):
                            chain(v.tensor_tensor(v4(g_cw)[:, a, 0, :], v4(g_cw)[:, a, 0, :], g_mask, ALU.mult))
                        for a in range(2):
                            for b in range(2):
                                o = (2 * a + b) * TAPS
                                v.tensor_tensor(g_coef[:, o:o + TAPS], v4(g_cw)[:, a, 0, :],
                                                v4(g_cw)[:, b, 1, :], ALU.mult)
                                last = v.scalar_tensor_tensor(out=g_fidx[:, o:o + TAPS], in0=v4(g_cor)[:, a, 0, :],
                                                              scalar=float(W), in1=v4(g_cor)[:, b, 1, :],
                                                              op0=ALU.mult, op1=ALU.add)
                        chain(last)
                        v.tensor_scalar(g_idx, g_fidx, float(i * HW), None, ALU.add).then_inc(m["idx"], 1)
                        for n in range(4):
                            dve.wait_ge(g_gather[i][n], (y + 1) * (16 * TAPS))
                            val = g_val[:, n * TAPS * C:(n + 1) * TAPS * C].rearrange("p (k c) -> p k c", c=C)
                            coef = g_coef[:, n * TAPS:(n + 1) * TAPS].rearrange("p (k o) -> p k o", o=1) \
                                .to_broadcast([P, TAPS, C])
                            dst = g_acc if n == 0 else g_tmp
                            chain(v.tensor_tensor(dst.rearrange("p (k c) -> p k c", c=C), val, coef, ALU.mult))
                            if n:
                                chain(v.tensor_tensor(g_acc, g_acc, g_tmp, ALU.add))
                        assert done[0] <= OWN
                        while done[0] < OWN:
                            done[0] += 1
                            dve.sem_inc(m["own"], 1)
                        dve.wait_ge(m["valT"], y + (at0 + 1))
                        v.tensor_copy(g_vT, pM[0:KS * C, 0:KS * W]).then_inc(m["copy"], 1)
                        dve.wait_ge(m["conv"], y + (at0 + 1))
                        v.scalar_tensor_tensor(out=g_out, in0=pV[0][0:C, 0:W], scalar=bias_s[0:C, 0:1], in1=g_x1,
                                               op0=ALU.add, op1=ALU.add).then_inc(m["out"], 1)

        @block.tensor
        def _(pe):
            mm = nc.tensor.matmul
            pe.wait_ge(const_ld, 16 * NCONST)
            for g in range(g_count):
                def add_rows(k, start, stop):
                    return mm(pD[g][:, :], ident[:, :], X[g][:, bass.ds(k * XCH, XCH)], start=start, stop=stop)
                for i in range(LOADS):
                    pe.wait_ge(x_ld[g][i], 16)
                    lo, hi = i * LOADCH, (i + 1) * LOADCH
                    if i == 0:
                        add_rows(0, True, False)
                        lo += 1
                    if i == LOADS - 1:
                        hi -= 1
                    with pe.Fori(lo, hi) as k:
                        add_rows(k, False, False)
                add_rows(NXC - 1, False, True).then_inc(colsum_done, 1)
            for g in range(g_count):
                pe.wait_ge(hat_done, 2 * g + 2)
                for d in range(2):
                    last = nc.tensor.transpose((pM, pR)[g][:, d * P:(d + 1) * P], hats[:, g, d, :], ident[:, :])
                last.then_inc(hatT_done, 1)
            for g in range(g_count):
                pe.wait_ge(rt_done, g + 1)
                for d in range(2):
                    for b in range(IPG):
                        o = d * P + b * 2 * MODES
                        last = mm(pH[g][0:C, o:o + 2 * MODES], rt[:, g, d, b * C:(b + 1) * C], dft_s[:, :],
                                  start=True, stop=True)
                last.then_inc(dft_done, 1)
            for g in range(g_count):
                pe.wait_ge(fs_done, g + 1)
                for d in range(2):
                    for f in range(MODES):
                        o = ((g * 2 + d) * MODES + f) * 2 * IPG
                        dst = pV[0][0:C, o:o + 2 * IPG]
                        for part in range(2):
                            w = wsp[:, 2 * d + part, :].rearrange("c (o f) -> c o f", f=MODES)[:, :, f]
                            src = fs[:, g, d, f, 1 - part:3 - part, :].rearrange("c a b -> c (a b)")
                            last = mm(dst, w, src, start=(part == 0), stop=(part == 1))
            last.then_inc(box_done, 1)
            pe.wait_ge(bx_done, 1)
            for g in range(g_count):
                for d in range(2):
                    for b in range(IPG):
                        o = (g * 2 + d) * P + b * C
                        last = nc.tensor.transpose(pV[1][0:2 * MODES, o:o + C], bx[:, g, d, b, :],
                                                   ident[0:C, 0:C])
            last.then_inc(boxT_done, 1)
            pe.wait_ge(bt_done, 1)
            for g in range(g_count):
                for d in range(2):
                    o = (g * 2 + d) * H
                    mm(pM[:, o:o + H], bt[:, g, d, :], inv_s[:, :], start=True, stop=True)
                last = mm(pR[:, g:g + 1], mwb[:, :], col1[:, g, 2:3], start=True, stop=True)
            last.then_inc(inv_done, 1)

            def mix(g, j, q):
                mm(pD[q][:, :], wm[:, g, :], X[g][:, bass.ds(j * (2 * XCH) + q * XCH, XCH)],
                   start=True, stop=True).then_inc(mix_done, 1)
            for g in range(g_count):
                first = 0
                if g == 0:
                    for q in range(2):
                        mix(g, 0, q)
                    first = 1
                with pe.Fori(first, NXC // 2) as j:
                    for q in range(2):
                        pe.wait_ge(x1_rows, j * 2 + (g * NXC + q - 1))
                        mix(g, j, q)
            pe.wait_ge(blocks_ld, 16 * NBLOCK)

            def step(g, s, q, on):
                N = s + g * NPAIR
                for c in range(NCH):
                    bp, k = divmod(c, TAPS)
                    pair = (2 * bp, 2 * bp + 1)
                    if on[1]:
                        n = N - 1
                        ci = n * NCH + c
                        wait(pe, abs_done, ci - 1)
                        if c == 0:
                            pe.wait_ge(hs_done, n * IPG + 2)
                        if c == TAPS:
                            pe.wait_ge(hs_done, n * IPG + 4)
                        for b in pair:
                            o = (b % 2) * PX
                            last = mm(pD[c % 2][:, o:o + PX], sdx_s[:, k, :], hs[:, b, 1 - q, :],
                                      start=True, stop=True)
                        last.then_inc(d_done, 1)
                        wait(pe, a_done, ci - 1)
                        for i in range(TILE_R):
                            for b in pair:
                                o = (b % 2) * PX + i * W
                                last = mm(pH[c % 2][:, o:o + W], shy_s[:, k, i, :],
                                          hs[:, b, 1 - q, i * W:(i + 1) * W], start=True, stop=True)
                        last.then_inc(h_done, 1)
                        if c in XT_AT:
                            t4 = XT_AT.index(c)
                            wait(pe, xt_done, n * 4 + t4)
                            if t4 == 0:
                                pe.wait_ge(wint_done, n + 1)
                            if t4 == 0 and on[0]:
                                pe.wait_ge(om_act, N + 1)
                            for u in range(4):
                                t = 4 * t4 + u
                                last = nc.tensor.transpose(
                                    pM[:, u * P:(u + 1) * P],
                                    wint[:, t * TILE_C:t * TILE_C + REG_C, :].rearrange("p x r -> p (x r)"),
                                    ident[:, :])
                            last.then_inc(t_done, 1)
                    if on[2] and c < NT:
                        n = N - 2
                        gi = next(i for i, tiles in enumerate(VGROUPS) if c in tiles)
                        tiles = VGROUPS[gi]
                        if c == 0:
                            pe.wait_ge(a_done, n * NCH + NCH)
                            pe.wait_ge(xt_done, n * 4 + 4)
                        if c == tiles[0]:
                            wait(pe, (v_act, v_dve)[gi % 2], n * 3 + gi // 2)
                        av = A[q].rearrange("p (k b i x) -> p b k i x", k=TAPS, b=IPG, i=TILE_R)
                        o = (c - tiles[0]) * TAPC
                        for b in range(IPG):
                            last = mm(pV[gi % 2][b * C:(b + 1) * C, o:o + TAPC],
                                      XT[q][:, c * P + b * C:c * P + (b + 1) * C],
                                      av[:, b, :, :, c * TILE_C:(c + 1) * TILE_C], start=True, stop=True)
                        if c == tiles[-1]:
                            last.then_inc(v_done, 1)
                    if on[2] and c == NCH - 1:
                        n = N - 2
                        pe.wait_ge(v_act, n * 3 + 3)
                        pe.wait_ge(v_dve, n * 3 + 3)
                        if on[0]:
                            pe.wait_ge(hy_abs, N * IPG + 4)
                            pe.wait_ge(hy_full, N * IPG + 4)
                        else:
                            pe.wait_ge(hy_full, (g + 1) * NPAIR * IPG)
                            wait(pe, out_ready, n)
                        vv = VS[q].rearrange("p (t k i j) -> p k i t j", t=NT, k=TAPS, i=TILE_R)
                        for t in range(TAPS):
                            last = mm(pR[:, 0:PX], wc[:, t, :], vv[:, t], start=(t == 0), stop=(t == TAPS - 1))
                        last.then_inc(conv_done, 1)
                    if on[0]:
                        if c == OM_AT:
                            wait(pe, xt_done, g * NPAIR * 4 if isinstance(s, int) and s == 0 else (N - 1) * 4)
                            pe.wait_ge(win_ld[q], (N - q) * 8 + 16)
                            for t in range(TAPS):
                                ky, kx = divmod(t, KS)
                                r, x0 = TOP - 1 + ky, LEFT - 1 + kx
                                last = mm(pM[0:OMG, 0:PX], wom[:, t, :],
                                          win[:, q, r:r + TILE_R, x0:x0 + W],
                                          start=(t == 0), stop=(t == TAPS - 1))
                            last.then_inc(om_done, 1)
                        if c in REP_AT:
                            b = REP_AT.index(c)
                            i = N * IPG + b
                            if b == 0:
                                pe.wait_ge(om_split, N + 1)
                                wait(pe, out_ready, N - 2 if on[3] else g * NPAIR)
                            wait(pe, hy_abs, i)
                            wait(pe, hy_full, i)
                            mm(pR[0:STK, 0:PX], seldy_s[:, b, :], om_hi[:, 0, :], start=True, stop=False)
                            mm(pR[0:STK, 0:PX], seldy_s[:, b, :], om_lo[:, 0, :], start=False, stop=True)
                            mm(pR[0:HYR, PX:2 * PX], selm_s[:, b, :], om_hi[:, 1, :], start=True, stop=False)
                            mm(pR[0:HYR, PX:2 * PX], selm_s[:, b, :], om_lo[:, 1, :], start=False,
                               stop=True).then_inc(rep_done, 1)
            steps(pe, step)

            pe.wait_ge(reach_col, 1)
            nc.tensor.transpose(pM[0:1, 0:OMG], rmax[:, :], ident[0:OMG, 0:OMG]).then_inc(reach_row, 1)
            pe.wait_ge(flag_set, 1)
            far = pe.value_load(flag_i[0:1, 0:1], min_val=0, max_val=1)
            with pe.If(far > 0):
                for g in range(g_count):
                    with pe.Fori(0, H) as r:
                        pe.wait_ge(g_row_ld, (r + (g * H + 1)) * 16)
                        nc.tensor.transpose(pM[:, 0:P], g_row, ident[:, :]).then_inc(g_row_T, 1)
                for i in range(images):
                    m = g_sem[i // IPG]
                    at0 = (i % IPG) * H
                    with pe.Fori(0, H) as y:
                        pe.wait_ge(m["load"], (y + (at0 + 1)) * 32)
                        for t in range(TAPS):
                            ky, kx = divmod(t, KS)
                            x0 = LEFT - 1 + kx
                            last = mm(pR[:, 0:OMC], g_win[:, ky, x0:x0 + W], wom[0:C, t, 0:OMC],
                                      start=(t == 0), stop=(t == TAPS - 1))
                        last.then_inc(m["om"], 1)
                        pe.wait_ge(m["own"], (y + (at0 + 1)) * OWN)
                        for j in range(KS):
                            last = nc.tensor.transpose(pM[0:KS * C, j * W:(j + 1) * W],
                                                       g_acc[:, j * KS * C:(j + 1) * KS * C], ident[:, :])
                        last.then_inc(m["valT"], 1)
                        pe.wait_ge(m["copy"], y + (at0 + 1))
                        for j in range(KS):
                            last = mm(pV[0][0:C, 0:W], g_wc[:, j, :], g_vT[:, j * W:(j + 1) * W],
                                      start=(j == 0), stop=(j == KS - 1))
                        last.then_inc(m["conv"], 1)


def constants():
    import numpy as np
    a = {}
    h = np.arange(H)
    f = np.arange(MODES)
    ang = 2 * np.pi * ((h[:, None] * f[None, :]) % H) / H
    a["dft"] = np.concatenate([np.cos(ang), -np.sin(ang)], 1).astype(np.float32)
    wgt = np.where(f == 0, 1.0, 2.0)[:, None] / H
    a["inv"] = np.concatenate([wgt * np.cos(ang.T), -wgt * np.sin(ang.T)], 0).astype(np.float32)
    a["inv"][MODES] = 0.0
    a["ident"] = np.eye(P, dtype=np.float32)
    seldy = np.zeros((OMG, IPG, STK), np.float16)
    selm = np.zeros((OMG, IPG, HYR), np.float16)
    sdx = np.zeros((P, TAPS, P), np.float16)
    shy = np.zeros((P, TAPS, TILE_R, P), np.float16)
    cols = np.zeros((P, 4), np.float32)
    cols[:, 3] = BN_EPS
    for b in range(IPG):
        for k in range(TAPS):
            for q in range(2):
                for s in range(NSH):
                    seldy[b * OMC + k, b, (q * NSH + s) * TAPS + k] = 1
                    selm[b * OMC + 2 * TAPS + k, b, (q * NSH + s) * TAPS + k] = 1
                seldy[b * OMC + TAPS + k, b, DX0 + q * TAPS + k] = 1
            cols[b * OMC + k, 2] = cols[b * OMC + TAPS + k, 2] = 3e38
    for q in range(2):
        for s in range(NSH):
            for k in range(TAPS):
                row = (q * NSH + s) * TAPS + k
                cols[row, 0] = REACH - s
                cols[row, 1] = -q
                for i in range(TILE_R):
                    r = i + k // KS + s + TOP - 1 - REACH
                    shy[row, k, i, r::REG_R] = 1
        for k in range(TAPS):
            cols[DX0 + q * TAPS + k, 1] = -q
            sdx[DX0 + q * TAPS + k, k, :] = 1
    col = np.arange(P) // REG_R
    for k in range(TAPS):
        sdx[POSR, k, :] = 1
        sdx[ONER, k, :] = (k % KS) - 1 + LEFT - col
    a["seldy"], a["selm"], a["sdx"], a["shy"], a["cols"] = seldy, selm, sdx, shy, cols
    hsc = np.ones((2, IPG, 2, PX), np.float16)
    hsc[0] = np.arange(PX) % TILE_C
    a["hsconst"] = hsc
    k = np.arange(TAPS)
    a["gtab"] = np.concatenate([np.broadcast_to(k // KS - 1.0, (P, TAPS)),
                                (k % KS - 1.0)[None, :] + np.arange(W)[:, None],
                                np.broadcast_to(np.arange(H) * 1.0, (P, H))], 1).astype(np.float32)
    return a


def kernel(x, L0_conv_w_x_r, L0_conv_w_x_i, L0_conv_w_y_r, L0_conv_w_y_i, L0_conv_mix_w, L0_conv_mix_b,
           L1_conv_w_om, L1_conv_b_om, L1_conv_weight, L1_conv_bias):
    import numpy as np
    import concourse.bacc as bacc
    from concourse.bass_utils import run_bass_kernel_spmd

    order = list(range(0, 2 * TAPS, 2)) + list(range(1, 2 * TAPS, 2)) + list(range(2 * TAPS, 3 * TAPS))
    arrays = {
        "x": x, "wxr": L0_conv_w_x_r, "wxi": L0_conv_w_x_i, "wyr": L0_conv_w_y_r, "wyi": L0_conv_w_y_i,
        "mixt": np.asarray(L0_conv_mix_w).T, "mixb": np.asarray(L0_conv_mix_b).reshape(C, 1),
        "womt": np.asarray(L1_conv_w_om)[order].reshape(OMC, C, TAPS).transpose(2, 1, 0),
        "bom": np.asarray(L1_conv_b_om)[order].reshape(OMC, 1),
        "wct": np.asarray(L1_conv_weight).reshape(C, C, TAPS).transpose(2, 1, 0),
        "biasc": np.asarray(L1_conv_bias).reshape(C, 1),
    }
    arrays.update({k: v for k, v in constants().items()})
    arrays = {k: np.ascontiguousarray(v) for k, v in arrays.items()}
    n = arrays["x"].shape[0]
    nc = bacc.Bacc("TRN2", target_bir_lowering=False, num_devices=1)
    names = ["x", "wxr", "wxi", "wyr", "wyi", "mixt", "mixb", "womt", "bom", "wct", "biasc",
             "dft", "inv", "ident", "seldy", "selm", "sdx", "shy", "hsconst", "cols", "gtab"]
    args = [nc.dram_tensor("in_" + k, arrays[k].shape, mybir.dt.from_np(arrays[k].dtype),
                           kind="ExternalInput").ap() for k in names]
    out = nc.dram_tensor("out", (n * C, HW), fp32, kind="ExternalOutput").ap()
    build(nc, n // IPG, *args, out)
    r = run_bass_kernel_spmd(nc, [{"in_" + k: arrays[k] for k in names}], core_ids=[0])
    return r.results[0]["out"].reshape(n, C, H, W)
```

```python
import concourse.bass as bass
from concourse import mybir
from contextlib import ExitStack

fp32 = mybir.dt.float32
fp16 = mybir.dt.float16
i32 = mybir.dt.int32
u32 = mybir.dt.uint32
ALU = mybir.AluOpType
ACT = mybir.ActivationFunctionType
AX = mybir.AxisListType

C = 32
H = W = 128
IPG = 4
P = IPG * C
HW = H * W
MODES = 16
KS = 3
TAPS = KS * KS
REACH = 2
NSH = 2 * REACH + 1
REG_R, REG_C = 8, 16
TILE_R, TILE_C = 2, 8
TOP, LEFT = 3, 4
PADR = TOP + H + TOP
PADC = LEFT + W + LEFT
NT = W // TILE_C
NPAIR = H // TILE_R
PX = TILE_R * W
OMC = 3 * TAPS
OMG = IPG * C
HYR = 2 * NSH * TAPS
DX0 = 96
STK = DX0 + 2 * TAPS
POSR, ONER = STK, STK + 1
NCH = 2 * TAPS
CH = 2 * PX
VGROUPS = [(0, 1, 2), (3, 4, 5), (6, 7, 8), (9, 10, 11), (12, 13), (14, 15)]
TAPC = TAPS * TILE_R * TILE_C
LEAD = 2
OM_AT = 0
OM_EVAC, SPLIT_AT, FLAG_AT = 2, 2, 3
WINT_AT = 1
V_AT = 2
XT_AT = (4, 6, 8, 10)
REP_AT = (6, 9, 12, 15)
HAT_LAG, STACK_LAG = 1, 2
CONV_AT = 12
OUT_AT = 15
UNROLL = 2
NV2 = IPG * KS
BN_EPS = 1e-5
XCH = 512
NXC = HW // XCH
RPC = XCH // W
LOADS = 8
XHR = 8


def build(nc, g_count, x, wxr, wxi, wyr, wyi, mixt, mixb, womt, bom, wct, biasc,
          dft, inv, ident_d, seldy, selm, sdx, shy, hsconst, cols, gtab, out):
    ctx = ExitStack()
    with ctx:
        def sb(name, shape, dt=fp32):
            return ctx.enter_context(nc.sbuf_tensor(name, shape, dt))

        def pb(name, shape, dt=fp32):
            return ctx.enter_context(nc.psum_tensor(name, shape, dt))

        def sem(name):
            return ctx.enter_context(nc.semaphore(name))

        x1_d = nc.dram_tensor("x1_scratch", (g_count * P, HW), fp32, kind="Internal").ap()
        xh_d = nc.dram_tensor("xh_scratch", (g_count * P, PADR * PADC), fp32, kind="Internal").ap()
        xt_d = nc.dram_tensor("xt_scratch", (g_count * IPG * HW, C), fp32, kind="Internal").ap()

        AW = TAPS * IPG * PX
        VW = NT * TAPC
        OMW = IPG * TILE_R * PADC
        sizes = [AW, AW, VW, VW, NT * P, NT * P, 3 * CH, 3 * CH, 2 * OMW]
        big = sb("big", [P, max(2 * HW, sum(sizes))])
        areas = [big[:, sum(sizes[:i]):sum(sizes[:i + 1])] for i in range(len(sizes))]
        X = [big[:, g * HW:(g + 1) * HW] for g in range(g_count)]
        A, VS, XT = areas[0:2], areas[2:4], areas[4:6]
        ub, vb = [a.rearrange("p (s n) -> p s n", s=3) for a in areas[6:8]]
        wino = areas[8].rearrange("p (s b r x) -> p s b r x", s=2, b=IPG, r=TILE_R)
        ident = sb("ident", [P, P])
        dft_s = sb("dft_s", [H, 2 * MODES])
        inv_s = sb("inv_s", [2 * MODES, H])
        wsp = sb("wsp", [C, 4, C * MODES])
        mwb = sb("mwb", [P, P])
        mixb_s = sb("mixb_s", [P, 1])
        wom = sb("wom", [KS * C, KS, C])
        bom_s = sb("bom_s", [OMG, 1])
        wc = sb("wc", [KS * C, KS, C])
        v2 = sb("v2", [KS * C, IPG, KS, PX])
        bias_s = sb("bias_s", [P, 1])
        seldy_s = sb("seldy_s", [OMG, IPG, STK], fp16)
        selm_s = sb("selm_s", [OMG, IPG, HYR], fp16)
        sdx_s = sb("sdx_s", [P, TAPS, P], fp16)
        shy_s = sb("shy_s", [P, TAPS, TILE_R, P], fp16)
        cols_s = sb("cols_s", [P, 4])
        stats = sb("stats", [P, NXC, 6])
        mv = sb("mv", [P, 2, 2])
        col1 = sb("col1", [P, 2, 8])
        sums = sb("sums", [P, 2, 2, H])
        hats = sb("hats", [P, 2, 2, H])
        rt = sb("rt", [H, 2, 2, P])
        fs = sb("fs", [C, 2, 2, MODES, 3, IPG])
        bx = sb("bx", [C, 2, 2, IPG, 2 * MODES])
        bt = sb("bt", [2 * MODES, 2, 2, P])
        xx = sb("xx", [P, 2, 2, H])
        wm = sb("wm", [P, 2, P])
        wint = sb("wint", [P, PADC, REG_R])
        zero = sb("zero", [P, TOP * PADC])
        win = sb("win", [P, 2, REG_R, PADC])
        stg = win
        x1r = sb("x1r", [P, 2, PX])
        outs = sb("outs", [P, 2, PX])
        om_s = sb("om_s", [OMG, 2, PX])
        om_hi = sb("om_hi", [OMG, 2, PX], fp16)
        om_lo = sb("om_lo", [OMG, 2, PX], fp16)
        reach = sb("reach", [OMG, PX])
        hy_u = sb("hy_u", [HYR, PX])
        hy_v = sb("hy_v", [HYR, PX])
        hy_f = sb("hy_f", [STK, PX])
        hy_h = sb("hy_h", [STK, PX], fp16)
        hs = sb("hs", [P, IPG, 2, PX], fp16)
        flag = sb("flag", [1, 2])
        flag_i = sb("flag_i", [1, 1], i32)
        rmax = sb("rmax", [OMG, 1])

        at = [0]

        def take(rows, n, dt=fp32):
            t = big[0:rows, at[0]:at[0] + n]
            at[0] += n
            return t if dt == fp32 else t.bitcast(dt)

        g_row = take(P, W)
        g_rowT = take(P, P)
        g_tab = take(P, 2 * TAPS + H)
        g_bom = take(P, OMC)
        g_wom = take(C, TAPS * OMC).rearrange("p (k m) -> p k m", k=TAPS)
        g_wc = take(KS * C, KS * C).rearrange("p (j o) -> p j o", j=KS)
        g_win = take(C, KS * PADC).rearrange("p (r x) -> p r x", r=KS)
        g_x1 = take(C, W)
        g_om = take(P, OMC)
        g_mask = take(P, TAPS)
        g_pos = take(P, 2 * TAPS)
        g_int = take(P, 2 * TAPS, i32)
        g_flo = take(P, 2 * TAPS)
        g_gt = take(P, 2 * TAPS)
        g_cor = take(P, 4 * TAPS)
        g_cw = take(P, 4 * TAPS)
        g_ok = take(P, 4 * TAPS)
        g_in = take(P, 4 * TAPS)
        g_coef = take(P, 4 * TAPS)
        g_fidx = take(P, 4 * TAPS)
        g_idx = take(P, 4 * TAPS, u32)
        g_val = take(P, 4 * TAPS * C)
        g_tmp = take(P, TAPS * C)
        g_acc = take(P, TAPS * C)
        g_vT = take(KS * C, KS * W)
        g_out = take(C, W)

        pD = [pb(f"pD{i}", [P, 512]) for i in range(2)]
        pH = [pb(f"pH{i}", [P, 512]) for i in range(2)]
        pV = [pb(f"pV{i}", [P, 512]) for i in range(2)]
        pM = pb("pM", [P, 512])
        pR = pb("pR", [P, 512])

        ident_ld = sem("ident_ld")
        const_ld = sem("const_ld")
        zeroed = sem("zeroed")
        blocks_ld = sem("blocks_ld")
        x_ld = [[sem(f"x_ld{g}_{i}") for i in range(LOADS)] for g in range(g_count)]
        stats_done = sem("stats_done")
        colsum_done = sem("colsum_done")
        aggr = sem("aggr")
        sd_done = sem("sd_done")
        dve_own = sem("dve_own")
        hat_done = sem("hat_done")
        hatT_done = sem("hatT_done")
        rt_done = sem("rt_done")
        dft_done = sem("dft_done")
        fs_done = sem("fs_done")
        box_done = sem("box_done")
        bx_done = sem("bx_done")
        boxT_done = sem("boxT_done")
        bt_done = sem("bt_done")
        inv_done = sem("inv_done")
        terms_done = sem("terms_done")
        mix_done = sem("mix_done")
        x1_rows = sem("x1_rows")
        x1_done = sem("x1_done")
        x1_st = sem("x1_st")
        norm1 = sem("norm1")
        xh_done = sem("xh_done")
        xh_st = [sem(f"xh_st{i}") for i in range(2)]
        pad_st = sem("pad_st")
        win_ld = [sem(f"win_ld{i}") for i in range(2)]
        wino_ld = [sem(f"wino_ld{i}") for i in range(2)]
        v2_ld = sem("v2_ld")
        x1_ld = [sem(f"x1_ld{i}") for i in range(2)]
        out_st = [sem(f"out_st{i}") for i in range(2)]
        wint_done = sem("wint_done")
        om_done = sem("om_done")
        om_act = sem("om_act")
        om_hi_done = sem("om_hi_done")
        om_split = sem("om_split")
        flag_done = sem("flag_done")
        rep_done = sem("rep_done")
        hy_abs = sem("hy_abs")
        hy_lin = sem("hy_lin")
        hy_full = sem("hy_full")
        hy_half = sem("hy_half")
        hs_done = sem("hs_done")
        d_done = sem("d_done")
        h_done = sem("h_done")
        abs_done = sem("abs_done")
        lin_done = sem("lin_done")
        a_done = sem("a_done")
        t_done = sem("t_done")
        xt_done = sem("xt_done")
        v_done = sem("v_done")
        v_act = sem("v_act")
        v_dve = sem("v_dve")
        conv_done = sem("conv_done")
        out_ready = sem("out_ready")
        reach_col = sem("reach_col")
        reach_row = sem("reach_row")
        flag_set = sem("flag_set")

        g_const = sem("g_const")
        g_row_ld = sem("g_row_ld")
        g_row_T = sem("g_row_T")
        g_row_copied = sem("g_row_copied")
        g_row_st = sem("g_row_st")
        g_ready = sem("g_ready")
        images = g_count * IPG
        kinds = ("load", "om", "act", "idx", "valT", "copy", "conv", "out", "store", "own")
        g_sem = [{k: sem(f"g_{k}{g}") for k in kinds} for g in range(g_count)]
        g_gather = [[sem(f"g_gather{i}_{m}") for m in range(4)] for i in range(images)]
        OWN = 31

        NCONST = 12
        NBLOCK = 4 * IPG + 2 * KS
        N_XH = H // XHR
        PAIRS = g_count * NPAIR
        LOADROWS = H // LOADS
        LOADCH = NXC // LOADS

        def wait(eng, s, v):
            if not (isinstance(v, int) and v <= 0):
                eng.wait_ge(s, v)

        def steps(eng, step):
            def peeled(first, end):
                for N in range(first, end):
                    step(N, N % 2, [0 <= N - k < PAIRS for k in range(4)], lambda n: divmod(n, NPAIR))
            peeled(0, 4)
            for g in range(g_count):
                first, loops = g * NPAIR + 4, (NPAIR - 5) // UNROLL
                with eng.Fori(0, loops) as j:
                    for q in range(UNROLL):
                        step(j * UNROLL + (first + q), q % 2, [True] * 4,
                             lambda n, g=g: (g, n - g * NPAIR))
                peeled(first + loops * UNROLL, (g + 1) * NPAIR + (4 if g + 1 < g_count else 3))

        def evacuate(q, gi):
            tiles = VGROUPS[gi]
            n = len(tiles)
            dst = VS[q].rearrange("p (k t n) -> p t k n", k=TAPS, t=NT)[:, tiles[0]:tiles[0] + n]
            return dst, pV[gi % 2][:, 0:n * TAPC].rearrange("p (t k n) -> p t k n", t=n, k=TAPS)

        def lead(on, N, q, c):
            if c + LEAD < NCH:
                return (N - 1, 1 - q, c + LEAD) if on[1] else None
            return (N, q, c + LEAD - NCH) if on[0] else None

        block = ctx.enter_context(nc.Block())

        @block.sync
        def _(sp):
            def load_images(g):
                xg = x[g * IPG:(g + 1) * IPG].rearrange("b c h w -> (b c) (h w)")
                for i in range(LOADS):
                    lo, hi = i * LOADROWS * W, (i + 1) * LOADROWS * W
                    sp.dma_start(X[g][:, lo:hi], xg[:, lo:hi]).then_inc(x_ld[g][i], 16)

            sp.dma_start(ident[:, :], ident_d).then_inc(ident_ld, 16)
            load_images(0)
            for dst, src in ((dft_s[:, :], dft), (inv_s[:, :], inv),
                             (wsp[:, 0, :], wxr.rearrange("c o f -> c (o f)")),
                             (wsp[:, 1, :], wxi.rearrange("c o f -> c (o f)")),
                             (wsp[:, 2, :], wyr.rearrange("c o f -> c (o f)")),
                             (wsp[:, 3, :], wyi.rearrange("c o f -> c (o f)")),
                             (cols_s[:, :], cols),
                             (seldy_s[:, :, :], seldy), (selm_s[:, :, :], selm),
                             (sdx_s[:, :, :], sdx), (shy_s[:, :, :, :], shy)):
                sp.dma_start(dst, src).then_inc(const_ld, 16)
            for g in range(1, g_count):
                load_images(g)
            sp.wait_ge(zeroed, 1)
            for b in range(IPG):
                r, m = slice(b * C, (b + 1) * C), slice(b * C, b * C + OMC)
                sp.dma_start(mwb[r, r], mixt).then_inc(blocks_ld, 16)
                sp.dma_start(mixb_s[r, :], mixb).then_inc(blocks_ld, 16)
                sp.dma_start(bom_s[m, :], bom).then_inc(blocks_ld, 16)
                sp.dma_start(bias_s[r, :], biasc).then_inc(blocks_ld, 16)
            for ky in range(KS):
                r, k = slice(ky * C, (ky + 1) * C), slice(ky * KS, (ky + 1) * KS)
                sp.dma_start(wom[r, :, 0:OMC], womt[k].rearrange("k c m -> c k m")).then_inc(blocks_ld, 16)
                sp.dma_start(wc[r, :, :], wct[k].rearrange("k c o -> c k o")).then_inc(blocks_ld, 16)
            sp.dma_start(hs[POSR:POSR + 2, :, :, :], hsconst).then_inc(const_ld, 16)
            for g in range(g_count):
                for edge in (0, TOP + H):
                    sp.dma_start(xh_d[g * P:(g + 1) * P, edge * PADC:(edge + TOP) * PADC],
                                 zero[:, :]).then_inc(pad_st, 16)
            for g in range(g_count):
                for i in range(LOADS):
                    lo, hi = i * LOADROWS * W, (i + 1) * LOADROWS * W
                    sp.wait_ge(x1_done, g * NXC + (i + 1) * LOADCH)
                    sp.dma_start(x1_d[g * P:(g + 1) * P, lo:hi], X[g][:, lo:hi]).then_inc(x1_st, 16)
                with sp.Fori(0, N_XH // 2) as j:
                    for q in range(2):
                        sp.wait_ge(xh_done, j * 2 + (g * N_XH + q + 1))
                        sp.dma_start(xh_d[g * P:(g + 1) * P,
                                          bass.ds(j * (2 * XHR * PADC) + (TOP + q * XHR) * PADC, XHR * PADC)],
                                     stg[:, q, :, :].rearrange("p a b -> p (a b)")).then_inc(xh_st[q], 16)
            sp.wait_ge(pad_st, 16 * 2 * g_count)
            sp.wait_ge(x1_st, 16 * LOADS * g_count)
            for q in range(2):
                sp.wait_ge(xh_st[q], 16 * (N_XH // 2) * g_count)

            def load_window(n, q, place):
                g, local = place(n)
                wait(sp, wint_done, n - 1)
                src = local * (TILE_R * PADC)
                sp.dma_start(win[:, q, :, :].rearrange("p a b -> p (a b)"),
                             xh_d[g * P:(g + 1) * P, bass.ds(src, REG_R * PADC)]).then_inc(win_ld[q], 16)
                wait(sp, om_done, n - 1)
                for ky in range(KS):
                    rows = xh_d[g * P:(g + 1) * P, bass.ds(src + (TOP - 1 + ky) * PADC, TILE_R * PADC)]
                    sp.dma_start(wino[ky * C:(ky + 1) * C, q, :, :, :].rearrange("c b r x -> c b (r x)"),
                                 rows.rearrange("(b c) n -> c b n", b=IPG)).then_inc(wino_ld[q], 16)

            def step(N, q, on, place):
                if isinstance(N, int) and N == 0:
                    load_window(0, 0, place)
                if not isinstance(N, int) or N + 1 < PAIRS:
                    load_window(N + 1, 1 - q, place)
                if on[3]:
                    g, local = place(N - 3)
                    sp.wait_ge(out_ready, N - 2)
                    sp.dma_start(out[g * P:(g + 1) * P, bass.ds(local * PX, PX)], outs[:, 1 - q, :]) \
                        .then_inc(out_st[1 - q], 16)
                if on[1]:
                    g, local = place(N - 1)
                    wait(sp, out_ready, N - 2)
                    sp.dma_start(x1r[:, 1 - q, :], x1_d[g * P:(g + 1) * P, bass.ds(local * PX, PX)]) \
                        .then_inc(x1_ld[1 - q], 16)
                if on[2]:
                    sp.wait_ge(v_act, (N - 1) * 3)
                    sp.wait_ge(v_dve, (N - 1) * 3)
                    wait(sp, conv_done, N - 2)
                    for b in range(IPG):
                        for ky in range(KS):
                            sp.dma_start(v2[ky * C:(ky + 1) * C, b, :, :].rearrange("c k n -> c (k n)"),
                                         VS[q][b * C:(b + 1) * C, ky * KS * PX:(ky + 1) * KS * PX]) \
                                .then_inc(v2_ld, 16)
            steps(sp, step)
            for q in range(2):
                sp.wait_ge(out_st[q], 16 * (NPAIR // 2) * g_count)

            sp.wait_ge(flag_set, 1)
            far = sp.value_load(flag_i[0:1, 0:1], min_val=0, max_val=1)
            with sp.If(far > 0):
                sp.dma_start(g_tab, gtab).then_inc(g_const, 16)
                sp.dma_start(g_bom, bom.rearrange("m o -> o m").to_broadcast([P, OMC])).then_inc(g_const, 16)
                sp.dma_start(g_wom, womt.rearrange("k c m -> c k m")).then_inc(g_const, 16)
                sp.dma_start(g_wc, wct.rearrange("(j k) c o -> (k c) j o", j=KS)).then_inc(g_const, 16)
                for g in range(g_count):
                    xt_v = xt_d[g * IPG * HW:(g + 1) * IPG * HW, :].rearrange("(i y x) c -> x y i c", i=IPG, y=H)
                    with sp.Fori(0, H) as r:
                        sp.dma_start(g_row, xh_d[g * P:(g + 1) * P, bass.ds(r * PADC + (TOP * PADC + LEFT), W)]) \
                            .then_inc(g_row_ld, 16)
                        sp.wait_ge(g_row_copied, r + (g * H + 1))
                        sp.nop(nofuse=True)
                        sp.dma_start(xt_v[:, bass.ds(r, 1), :, :].rearrange("x y i c -> x (y i) c"),
                                     g_rowT.rearrange("p (i c) -> p i c", i=IPG)).then_inc(g_row_st, 16)
                        sp.wait_ge(g_row_st, (r + (g * H + 1)) * 16)
                        sp.nop(nofuse=True)
                sp.sem_inc(g_ready, 1)
                for i in range(images):
                    m = g_sem[i // IPG]
                    at0 = (i % IPG) * H
                    with sp.Fori(0, H) as y:
                        sp.dma_start(g_win.rearrange("p r x -> p (r x)"),
                                     xh_d[i * C:(i + 1) * C, bass.ds(y * PADC + (TOP - 1) * PADC, KS * PADC)]) \
                            .then_inc(m["load"], 16)
                        sp.dma_start(g_x1, x1_d[i * C:(i + 1) * C, bass.ds(y * W, W)]).then_inc(m["load"], 16)
                        sp.wait_ge(m["out"], y + (at0 + 1))
                        sp.nop(nofuse=True)
                        sp.dma_start(out[i * C:(i + 1) * C, bass.ds(y * W, W)], g_out).then_inc(m["store"], 16)
                        sp.wait_ge(m["store"], (y + (at0 + 1)) * 16)
                        sp.nop(nofuse=True)

        @block.gpsimd
        def _(pool):
            for t in (mwb[:, :], wom[:, :, :], bom_s[:, :], zero[:, :], stg[:, :, :, :],
                      reach[:, :], hy_f[:, :], hs[:, :, :, :]):
                last = nc.gpsimd.memset(t, 0.0)
            last.then_inc(zeroed, 1)

            def step(N, q, on, place):
                for c in range(NCH):
                    ahead = lead(on, N, q, c)
                    if ahead:
                        n, qn, cn = ahead
                        ci = n * NCH + cn
                        pool.wait_ge(abs_done, ci + 1)
                        wait(pool, a_done, ci - 2)
                        pool.nop(nofuse=True)
                        nc.gpsimd.tensor_scalar(vb[:, cn % 3, :], ub[:, cn % 3, :], -1.0, 1.0,
                                                ALU.mult, ALU.add).then_inc(lin_done, 1)
                    if on[0]:
                        if c == SPLIT_AT:
                            pool.wait_ge(om_hi_done, N + 1)
                            nc.gpsimd.tensor_tensor(om_lo[:, :, :], om_s[:, :, :], om_hi[:, :, :],
                                                    ALU.subtract).then_inc(om_split, 1)
                        if c in REP_AT:
                            k = N * IPG + REP_AT.index(c)
                            pool.wait_ge(hy_abs, k + 1)
                            wait(pool, hy_full, k)
                            pool.nop(nofuse=True)
                            nc.gpsimd.tensor_scalar(hy_v[:, :], hy_u[:, :], -1.0, 1.0,
                                                    ALU.mult, ALU.add).then_inc(hy_lin, 1)
            steps(pool, step)

            pool.wait_ge(flag_set, 1)
            far = pool.value_load(flag_i[0:1, 0:1], min_val=0, max_val=1)
            with pool.If(far > 0):
                pool.wait_ge(g_ready, 1)
                for i in range(images):
                    m = g_sem[i // IPG]
                    at0 = (i % IPG) * H
                    with pool.Fori(0, H) as y:
                        pool.wait_ge(m["idx"], y + (at0 + 1))
                        pool.nop(nofuse=True)
                        for k in range(4 * TAPS):
                            nc.gpsimd.indirect_dma_start(
                                out=g_val[:, k * C:(k + 1) * C], out_offset=None, in_=xt_d,
                                in_offset=bass.IndirectOffsetOnAxis(ap=g_idx[:, k:k + 1], axis=0)) \
                                .then_inc(g_gather[i][k // TAPS], 16)
                        pool.wait_ge(m["valT"], y + (at0 + 1))
                        pool.nop(nofuse=True)


        @block.scalar
        def _(act):
            act.wait_ge(const_ld, 16 * NCONST)
            def deviation(g, n):
                act.wait_ge(aggr, n * g_count + g + 1)
                nc.scalar.activation(col1[:, g, 5 * n:5 * n + 1], mv[:, g, 1:2], ACT.Sqrt,
                                     bias=cols_s[:, 3:4]).then_inc(sd_done, 1)

            for g in range(g_count):
                deviation(g, 0)
            act.wait_ge(zeroed, 1)

            def normalize(g, j, q):
                nc.scalar.activation(
                    stg[:, q, :, LEFT:LEFT + W],
                    X[g][:, bass.ds(j * (2 * XHR * W) + q * XHR * W, XHR * W)]
                    .rearrange("p (a b) -> p a b", b=W),
                    ACT.Identity, bias=col1[:, g, 7:8], scale=col1[:, g, 6:7]).then_inc(xh_done, 1)

            for g in range(g_count):
                deviation(g, 1)
                act.wait_ge(norm1, g + 1)
                first = 0
                if g == 0:
                    for q in range(2):
                        normalize(g, 0, q)
                    first = 1
                with act.Fori(first, N_XH // 2) as j:
                    for q in range(2):
                        act.wait_ge(xh_st[q], (j + g * (N_XH // 2)) * 16)
                        normalize(g, j, q)
            act.wait_ge(x1_st, 16 * LOADS * g_count)
            act.wait_ge(blocks_ld, 16 * NBLOCK)

            def step(N, q, on, place):
                for c in range(NCH):
                    ahead = lead(on, N, q, c)
                    if ahead:
                        n, qn, cn = ahead
                        ci = n * NCH + cn
                        act.wait_ge(d_done, ci + 1)
                        wait(act, lin_done, ci - 2)
                        nc.scalar.activation(ub[:, cn % 3, :], pD[cn % 2][:, :], ACT.Abs) \
                            .then_inc(abs_done, 1)
                    if on[1] and c == WINT_AT:
                        n = N - 1
                        act.wait_ge(win_ld[1 - q], (n - (1 - q)) * 8 + 16)
                        wait(act, t_done, n * 4)
                        nc.scalar.activation(wint[:, :, :].rearrange("p x r -> p r x"), win[:, 1 - q, :, :],
                                             ACT.Copy).then_inc(wint_done, 1)
                    if on[1]:
                        if c in XT_AT:
                            k = XT_AT.index(c)
                            act.wait_ge(t_done, (N - 1) * 4 + (k + 1))
                            if k == 0:
                                wait(act, v_done, (N - 2) * len(VGROUPS))
                            nc.scalar.activation(XT[1 - q][:, k * 512:(k + 1) * 512], pM[:, :],
                                                 ACT.Copy).then_inc(xt_done, 1)
                    if on[2]:
                        for gi, tiles in enumerate(VGROUPS):
                            if gi % 2 == 0 and tiles[-1] == c - V_AT:
                                act.wait_ge(v_done, (N - 2) * len(VGROUPS) + (gi + 1))
                                if gi == 0:
                                    wait(act, v2_ld, (N - 3) * (16 * NV2))
                                nc.scalar.activation(*evacuate(q, gi), ACT.Copy).then_inc(v_act, 1)
                    if on[0]:
                        if c == OM_EVAC:
                            act.wait_ge(om_done, N + 1)
                            wait(act, om_split, N)
                            wait(act, flag_done, 2 * N)
                            nc.scalar.activation(om_s[:, 0, :], pM[0:OMG, 0:PX], ACT.Identity,
                                                 bias=bom_s[:, 0:1])
                            nc.scalar.activation(om_s[:, 1, :], pM[0:OMG, 0:PX], ACT.Sigmoid,
                                                 bias=bom_s[:, 0:1]).then_inc(om_act, 1)
                            act.wait_ge(om_act, N + 1)
                            wait(act, rep_done, N * IPG)
                            nc.scalar.activation(om_hi[:, :, :], om_s[:, :, :], ACT.Copy).then_inc(om_hi_done, 1)
                        if c in REP_AT:
                            k = N * IPG + REP_AT.index(c)
                            act.wait_ge(rep_done, k + 1)
                            wait(act, hy_lin, k)
                            wait(act, hs_done, k)
                            nc.scalar.activation(hy_u[:, :], pR[0:HYR, 0:PX], ACT.Abs,
                                                 bias=cols_s[0:HYR, 0:1])
                            nc.scalar.activation(hy_f[DX0:STK, :], pR[DX0:STK, 0:PX],
                                                 ACT.Copy).then_inc(hy_abs, 1)
            steps(act, step)

            act.wait_ge(flag_set, 1)
            far = act.value_load(flag_i[0:1, 0:1], min_val=0, max_val=1)
            with act.If(far > 0):
                for i in range(images):
                    m = g_sem[i // IPG]
                    at0 = (i % IPG) * H
                    with act.Fori(0, H) as y:
                        act.wait_ge(m["own"], y * OWN + (at0 * OWN + 1))
                        nc.scalar.activation(g_mask, g_om[:, 2 * TAPS:OMC], ACT.Sigmoid).then_inc(m["act"], 1)

        @block.vector
        def _(dve):
            own = [0]

            def link(ins):
                own[0] += 1
                ins.then_inc(dve_own, 1)
                dve.wait_ge(dve_own, own[0])

            for g in range(g_count):
                for i in range(LOADS):
                    dve.wait_ge(x_ld[g][i], 16)
                    with dve.Fori(i * LOADCH, (i + 1) * LOADCH) as k:
                        part = X[g][:, bass.ds(k * XCH, XCH)]
                        nc.vector.tensor_reduce(sums[:, g, 0, bass.ds(k * RPC, RPC)],
                                                part.rearrange("p (a b) -> p a b", b=W), AX.X, ALU.add)
                        nc.vector.bn_stats(stats[:, bass.ds(k, 1), :].rearrange("p a b -> p (a b)"),
                                           part).then_inc(stats_done, 1)
                dve.wait_ge(stats_done, (g + 1) * NXC)
                nc.vector.bn_aggr(mv[:, g, :], stats[:, :, :].rearrange("p a b -> p (a b)")).then_inc(aggr, 1)
                dve.wait_ge(aggr, g + 1)
            dve.wait_ge(ident_ld, 16)
            dve.wait_ge(const_ld, 16 * NCONST)
            dve.wait_ge(zeroed, 1)
            for g in range(g_count):
                dve.wait_ge(colsum_done, g + 1)
                link(nc.vector.tensor_reduce(sums[:, g, 1, :], pD[g][:, :].rearrange("p (r w) -> p w r", w=W),
                                             AX.X, ALU.add))
                dve.wait_ge(sd_done, g + 1)
                link(nc.vector.reciprocal(col1[:, g, 1:2], col1[:, g, 0:1]))
                link(nc.vector.scalar_tensor_tensor(out=col1[:, g, 2:3], in0=mv[:, g, 0:1], scalar=-1.0,
                                                    in1=col1[:, g, 1:2], op0=ALU.mult, op1=ALU.mult))
                link(nc.vector.tensor_scalar(col1[:, g, 3:4], col1[:, g, 1:2], 1.0 / W, None, ALU.mult))
                nc.vector.tensor_scalar(hats[:, g, :, :], sums[:, g, :, :], col1[:, g, 3:4],
                                        col1[:, g, 2:3], ALU.mult, ALU.add).then_inc(hat_done, 1)
                dve.wait_ge(blocks_ld, 16 * NBLOCK)
                nc.vector.scalar_tensor_tensor(out=wm[:, g, :], in0=mwb[:, :], scalar=col1[:, g, 1:2],
                                               in1=ident[:, :], op0=ALU.mult, op1=ALU.add).then_inc(hat_done, 1)
            for g in range(g_count):
                dve.wait_ge(hatT_done, g + 1)
                src = (pM, pR)[g]
                nc.vector.tensor_copy(rt[:, g, :, :].rearrange("p a b -> p (a b)"), src[:, 0:2 * P]) \
                    .then_inc(rt_done, 1)
            for g in range(g_count):
                dve.wait_ge(dft_done, g + 1)
                for d in range(2):
                    f = pH[g][0:C, d * P:(d + 1) * P].rearrange("c (b r f) -> c f b r", b=IPG, r=2)
                    nc.vector.tensor_copy(fs[:, g, d, :, 1, :], f[:, :, :, 0])
                    nc.vector.tensor_copy(fs[:, g, d, :, 2, :], f[:, :, :, 1])
                    last = nc.vector.tensor_scalar(fs[:, g, d, :, 0, :], f[:, :, :, 1], -1.0, None, ALU.mult)
                last.then_inc(fs_done, 1)
            dve.wait_ge(box_done, 1)
            for g in range(g_count):
                for d in range(2):
                    o = (g * 2 + d) * P
                    v = pV[0][0:C, o:o + P].rearrange("c (f r b) -> c b r f", f=MODES, r=2)
                    for b in range(IPG):
                        last = nc.vector.tensor_copy(bx[:, g, d, b, :].rearrange("c (r f) -> c r f", r=2),
                                                     v[:, b])
            last.then_inc(bx_done, 1)
            dve.wait_ge(boxT_done, 1)
            nc.vector.tensor_copy(bt[:, 0:g_count, :, :].rearrange("p a b c -> p (a b c)"),
                                  pV[1][0:2 * MODES, 0:g_count * 2 * P]).then_inc(bt_done, 1)
            dve.wait_ge(inv_done, 1)
            for g in range(g_count):
                link(nc.vector.tensor_tensor(col1[:, g, 4:5], pR[:, g:g + 1], mixb_s[:, :], ALU.add))
                nc.vector.tensor_scalar(xx[:, g, 0, :], pM[:, g * 2 * H:g * 2 * H + H], col1[:, g, 4:5],
                                        None, ALU.add)
                link(nc.vector.tensor_copy(xx[:, g, 1, :], pM[:, g * 2 * H + H:g * 2 * H + 2 * H]))

            for g in range(g_count):
                with dve.Fori(0, NXC // 2) as j:
                    for q in range(2):
                        k = j * 2 + q
                        dve.wait_ge(mix_done, k + (g * NXC + 1))
                        for r in range(RPC):
                            row = j * (2 * RPC) + (q * RPC + r)
                            last = nc.vector.scalar_tensor_tensor(
                                out=X[g][:, bass.ds(j * (2 * XCH) + (q * XCH + r * W), W)],
                                in0=pD[q][:, r * W:(r + 1) * W], scalar=xx[:, g, 0, bass.ds(row, 1)],
                                in1=xx[:, g, 1, :], op0=ALU.add, op1=ALU.add)
                        last.then_inc(x1_rows, 1)
                        dve.wait_ge(x1_rows, k + (g * NXC + 1))
                        nc.vector.bn_stats(stats[:, bass.ds(k, 1), :].rearrange("p a b -> p (a b)"),
                                           X[g][:, bass.ds(j * (2 * XCH) + q * XCH, XCH)]).then_inc(x1_done, 1)
                dve.wait_ge(x1_done, (g + 1) * NXC)
                dve.wait_ge(sd_done, g_count)
                nc.vector.bn_aggr(mv[:, g, :], stats[:, :, :].rearrange("p a b -> p (a b)")).then_inc(aggr, 1)
                dve.wait_ge(aggr, g_count + g + 1)
                dve.wait_ge(sd_done, g_count + g + 1)
                link(nc.vector.reciprocal(col1[:, g, 6:7], col1[:, g, 5:6]))
                nc.vector.scalar_tensor_tensor(out=col1[:, g, 7:8], in0=mv[:, g, 0:1], scalar=-1.0,
                                               in1=col1[:, g, 6:7], op0=ALU.mult, op1=ALU.mult).then_inc(norm1, 1)
            dve.wait_ge(x1_st, 16 * LOADS * g_count)
            dve.wait_ge(xh_done, N_XH * g_count)

            def step(N, q, on, place):
                for c in range(NCH):
                    bp, k = divmod(c, TAPS)
                    if on[1]:
                        ci = (N - 1) * NCH + c
                        dve.wait_ge(lin_done, ci + 1)
                        dve.wait_ge(h_done, ci + 1)
                        if c == 0:
                            wait(dve, v_done, (N - 2) * len(VGROUPS))
                        o = k * IPG * PX + bp * CH
                        nc.vector.scalar_tensor_tensor(out=A[1 - q][:, o:o + CH], in0=vb[:, c % 3, :],
                                                       scalar=0.0, in1=pH[c % 2][:, :],
                                                       op0=ALU.max, op1=ALU.mult).then_inc(a_done, 1)
                    if on[0] and c - HAT_LAG in REP_AT:
                        i = N * IPG + REP_AT.index(c - HAT_LAG)
                        dve.wait_ge(hy_lin, i + 1)
                        wait(dve, hs_done, i)
                        nc.vector.scalar_tensor_tensor(out=hy_f[0:HYR, :], in0=hy_v[:, :], scalar=0.0,
                                                       in1=pR[0:HYR, PX:2 * PX], op0=ALU.max,
                                                       op1=ALU.mult).then_inc(hy_full, 1)
                    if on[2]:
                        for gi, tiles in enumerate(VGROUPS):
                            if gi % 2 == 1 and tiles[-1] == c - V_AT:
                                dve.wait_ge(v_done, (N - 2) * len(VGROUPS) + (gi + 1))
                                if gi == 1:
                                    wait(dve, v2_ld, (N - 3) * (16 * NV2))
                                nc.vector.tensor_copy(*evacuate(q, gi)).then_inc(v_dve, 1)
                    if on[3] and c == OUT_AT:
                        n = N - 3
                        dve.wait_ge(conv_done, n + 1)
                        dve.wait_ge(x1_ld[1 - q], (n - (1 - q)) * 8 + 16)
                        m = (n - (1 - q)) * 8
                        if not (isinstance(m, int) and m == 0):
                            dve.wait_ge(out_st[1 - q], m)
                        nc.vector.scalar_tensor_tensor(out=outs[:, 1 - q, :], in0=pM[:, PX:2 * PX],
                                                       scalar=bias_s[:, 0:1], in1=x1r[:, 1 - q, :],
                                                       op0=ALU.add, op1=ALU.add).then_inc(out_ready, 1)
                    if on[0]:
                        if c == FLAG_AT:
                            dve.wait_ge(om_act, N + 1)
                            for i in range(2):
                                wait(dve, flag_done, 2 * N + i)
                                nc.vector.scalar_tensor_tensor(out=reach[:, :], in0=om_s[:, 0, :],
                                                               scalar=(1.0, -1.0)[i], in1=reach[:, :],
                                                               op0=ALU.mult, op1=ALU.max).then_inc(flag_done, 1)
                        if c - HAT_LAG in REP_AT:
                            b = REP_AT.index(c - HAT_LAG)
                            dve.wait_ge(hy_full, N * IPG + b + 1)
                            wait(dve, hs_done, N * IPG + b)
                            nc.vector.tensor_copy(hy_h[:, :], hy_f[:, :]).then_inc(hy_half, 1)
                        if c - STACK_LAG in REP_AT:
                            b = REP_AT.index(c - STACK_LAG)
                            dve.wait_ge(hy_half, N * IPG + b + 1)
                            if b == 0:
                                wait(dve, h_done, (N - 1) * NCH)
                            nc.vector.scalar_tensor_tensor(out=hs[0:STK, b, q, :], in0=hy_h[:, :],
                                                           scalar=cols_s[0:STK, 1:2], in1=hy_f[:, :],
                                                           op0=ALU.mult, op1=ALU.add).then_inc(hs_done, 1)
            steps(dve, step)

            dve.wait_ge(flag_done, 2 * NPAIR * g_count)
            link(nc.vector.tensor_reduce(rmax[:, :], reach[:, :], AX.X, ALU.max))
            nc.vector.tensor_tensor(rmax[:, :], rmax[:, :], cols_s[0:OMG, 2:3], ALU.min).then_inc(reach_col, 1)
            dve.wait_ge(reach_row, 1)
            link(nc.vector.tensor_reduce(flag[:, 0:1], pM[0:1, 0:OMG], AX.X, ALU.max))
            link(nc.vector.tensor_scalar(flag[:, 1:2], flag[:, 0:1], float(REACH), None, ALU.is_gt))
            nc.vector.tensor_copy(flag_i[:, :], flag[:, 1:2]).then_inc(flag_set, 1)
            dve.wait_ge(flag_set, 1)
            far = dve.value_load(flag_i[0:1, 0:1], min_val=0, max_val=1)
            with dve.If(far > 0):
                dve.wait_ge(g_const, 64)
                for g in range(g_count):
                    with dve.Fori(0, H) as r:
                        dve.wait_ge(g_row_T, r + (g * H + 1))
                        nc.vector.tensor_copy(g_rowT, pM[:, 0:P]).then_inc(g_row_copied, 1)

                def v4(t):
                    return t.rearrange("p (a d k) -> p a d k", a=2, d=2)

                for i in range(images):
                    m = g_sem[i // IPG]
                    at0 = (i % IPG) * H
                    with dve.Fori(0, H) as y:
                        done = [0]

                        def chain(ins):
                            done[0] += 1
                            ins.then_inc(m["own"], 1)
                            dve.wait_ge(m["own"], y * OWN + (at0 * OWN + done[0]))

                        v = nc.vector
                        dve.wait_ge(m["om"], y + (at0 + 1))
                        chain(v.tensor_tensor(g_om, pR[:, 0:OMC], g_bom, ALU.add))
                        chain(v.tensor_tensor(g_pos, g_om[:, 0:2 * TAPS], g_tab[:, 0:2 * TAPS], ALU.add))
                        chain(v.tensor_scalar(g_pos[:, 0:TAPS], g_pos[:, 0:TAPS],
                                              g_tab[:, bass.ds(y + 2 * TAPS, 1)], None, ALU.add))
                        chain(v.tensor_scalar(g_pos, g_pos, -2.0, float(H + 1), ALU.max, ALU.min))
                        chain(v.tensor_copy(g_int, g_pos))
                        chain(v.tensor_copy(g_flo, g_int))
                        chain(v.tensor_tensor(g_gt, g_flo, g_pos, ALU.is_gt))
                        chain(v.tensor_tensor(g_cor[:, 0:2 * TAPS], g_flo, g_gt, ALU.subtract))
                        chain(v.tensor_scalar(g_cor[:, 2 * TAPS:], g_cor[:, 0:2 * TAPS], 1.0, None, ALU.add))
                        chain(v.tensor_tensor(g_cw[:, 2 * TAPS:], g_pos, g_cor[:, 0:2 * TAPS], ALU.subtract))
                        chain(v.tensor_scalar(g_cw[:, 0:2 * TAPS], g_cw[:, 2 * TAPS:], -1.0, 1.0,
                                              ALU.mult, ALU.add))
                        chain(v.tensor_scalar(g_ok, g_cor, 0.0, None, ALU.is_ge))
                        chain(v.scalar_tensor_tensor(out=g_in, in0=g_cor, scalar=float(H - 1), in1=g_ok,
                                                     op0=ALU.is_le, op1=ALU.mult))
                        chain(v.tensor_tensor(g_cw, g_cw, g_in, ALU.mult))
                        chain(v.tensor_scalar(g_cor, g_cor, 0.0, float(H - 1), ALU.max, ALU.min))
                        dve.wait_ge(m["act"], y + (at0 + 1))
                        for a in range(2):
                            chain(v.tensor_tensor(v4(g_cw)[:, a, 0, :], v4(g_cw)[:, a, 0, :], g_mask, ALU.mult))
                        for a in range(2):
                            for b in range(2):
                                o = (2 * a + b) * TAPS
                                v.tensor_tensor(g_coef[:, o:o + TAPS], v4(g_cw)[:, a, 0, :],
                                                v4(g_cw)[:, b, 1, :], ALU.mult)
                                last = v.scalar_tensor_tensor(out=g_fidx[:, o:o + TAPS], in0=v4(g_cor)[:, a, 0, :],
                                                              scalar=float(W), in1=v4(g_cor)[:, b, 1, :],
                                                              op0=ALU.mult, op1=ALU.add)
                        chain(last)
                        v.tensor_scalar(g_idx, g_fidx, float(i * HW), None, ALU.add).then_inc(m["idx"], 1)
                        for n in range(4):
                            dve.wait_ge(g_gather[i][n], (y + 1) * (16 * TAPS))
                            val = g_val[:, n * TAPS * C:(n + 1) * TAPS * C].rearrange("p (k c) -> p k c", c=C)
                            coef = g_coef[:, n * TAPS:(n + 1) * TAPS].rearrange("p (k o) -> p k o", o=1) \
                                .to_broadcast([P, TAPS, C])
                            dst = g_acc if n == 0 else g_tmp
                            chain(v.tensor_tensor(dst.rearrange("p (k c) -> p k c", c=C), val, coef, ALU.mult))
                            if n:
                                chain(v.tensor_tensor(g_acc, g_acc, g_tmp, ALU.add))
                        assert done[0] <= OWN
                        while done[0] < OWN:
                            done[0] += 1
                            dve.sem_inc(m["own"], 1)
                        dve.wait_ge(m["valT"], y + (at0 + 1))
                        v.tensor_copy(g_vT, pM[0:KS * C, 0:KS * W]).then_inc(m["copy"], 1)
                        dve.wait_ge(m["conv"], y + (at0 + 1))
                        v.scalar_tensor_tensor(out=g_out, in0=pV[0][0:C, 0:W], scalar=bias_s[0:C, 0:1], in1=g_x1,
                                               op0=ALU.add, op1=ALU.add).then_inc(m["out"], 1)

        @block.tensor
        def _(pe):
            mm = nc.tensor.matmul
            pe.wait_ge(ident_ld, 16)
            for g in range(g_count):
                def add_rows(k, start, stop):
                    return mm(pD[g][:, :], ident[:, :], X[g][:, bass.ds(k * XCH, XCH)], start=start, stop=stop)
                for i in range(LOADS):
                    pe.wait_ge(x_ld[g][i], 16)
                    lo, hi = i * LOADCH, (i + 1) * LOADCH
                    if i == 0:
                        add_rows(0, True, False)
                        lo += 1
                    if i == LOADS - 1:
                        hi -= 1
                    with pe.Fori(lo, hi) as k:
                        add_rows(k, False, False)
                add_rows(NXC - 1, False, True).then_inc(colsum_done, 1)
            pe.wait_ge(const_ld, 16 * NCONST)
            for g in range(g_count):
                pe.wait_ge(hat_done, 2 * g + 2)
                for d in range(2):
                    last = nc.tensor.transpose((pM, pR)[g][:, d * P:(d + 1) * P], hats[:, g, d, :], ident[:, :])
                last.then_inc(hatT_done, 1)
            for g in range(g_count):
                pe.wait_ge(rt_done, g + 1)
                for d in range(2):
                    for b in range(IPG):
                        o = d * P + b * 2 * MODES
                        last = mm(pH[g][0:C, o:o + 2 * MODES], rt[:, g, d, b * C:(b + 1) * C], dft_s[:, :],
                                  start=True, stop=True)
                last.then_inc(dft_done, 1)
            for g in range(g_count):
                pe.wait_ge(fs_done, g + 1)
                for d in range(2):
                    for f in range(MODES):
                        o = ((g * 2 + d) * MODES + f) * 2 * IPG
                        dst = pV[0][0:C, o:o + 2 * IPG]
                        for part in range(2):
                            w = wsp[:, 2 * d + part, :].rearrange("c (o f) -> c o f", f=MODES)[:, :, f]
                            src = fs[:, g, d, f, 1 - part:3 - part, :].rearrange("c a b -> c (a b)")
                            last = mm(dst, w, src, start=(part == 0), stop=(part == 1))
            last.then_inc(box_done, 1)
            pe.wait_ge(bx_done, 1)
            for g in range(g_count):
                for d in range(2):
                    for b in range(IPG):
                        o = (g * 2 + d) * P + b * C
                        last = nc.tensor.transpose(pV[1][0:2 * MODES, o:o + C], bx[:, g, d, b, :],
                                                   ident[0:C, 0:C])
            last.then_inc(boxT_done, 1)
            pe.wait_ge(bt_done, 1)
            for g in range(g_count):
                for d in range(2):
                    o = (g * 2 + d) * H
                    mm(pM[:, o:o + H], bt[:, g, d, :], inv_s[:, :], start=True, stop=True)
                last = mm(pR[:, g:g + 1], mwb[:, :], col1[:, g, 2:3], start=True, stop=True)
            last.then_inc(inv_done, 1)

            def mix(g, j, q):
                mm(pD[q][:, :], wm[:, g, :], X[g][:, bass.ds(j * (2 * XCH) + q * XCH, XCH)],
                   start=True, stop=True).then_inc(mix_done, 1)
            for g in range(g_count):
                first = 0
                if g == 0:
                    for q in range(2):
                        mix(g, 0, q)
                    first = 1
                with pe.Fori(first, NXC // 2) as j:
                    for q in range(2):
                        pe.wait_ge(x1_rows, j * 2 + (g * NXC + q - 1))
                        mix(g, j, q)
            pe.wait_ge(blocks_ld, 16 * NBLOCK)

            def step(N, q, on, place):
                for c in range(NCH):
                    bp, k = divmod(c, TAPS)
                    ahead = lead(on, N, q, c)
                    if ahead:
                        n, qn, cn = ahead
                        wait(pe, abs_done, n * NCH + cn - 1)
                        if cn == 0:
                            pe.wait_ge(hs_done, n * IPG + 2)
                        if cn == TAPS:
                            pe.wait_ge(hs_done, n * IPG + 4)
                        b = 2 * (cn // TAPS)
                        mm(pD[cn % 2][:, :], sdx_s[:, cn % TAPS, :], hs[:, b:b + 2, qn, :],
                           start=True, stop=True).then_inc(d_done, 1)
                    if on[1]:
                        n = N - 1
                        ci = n * NCH + c
                        wait(pe, a_done, ci - 1)
                        for i in range(TILE_R):
                            last = mm(pH[c % 2][:, :].rearrange("p (b i x) -> p b i x", b=2, i=TILE_R)[:, :, i, :],
                                      shy_s[:, k, i, :], hs[:, 2 * bp:2 * bp + 2, 1 - q, i * W:(i + 1) * W],
                                      start=True, stop=True)
                        last.then_inc(h_done, 1)
                        if c in XT_AT:
                            t4 = XT_AT.index(c)
                            wait(pe, xt_done, n * 4 + t4)
                            if t4 == 0:
                                pe.wait_ge(wint_done, n + 1)
                                pe.wait_ge(om_act, N + 1 if on[0] else PAIRS)
                                wait(pe, out_ready, N - 3)
                            for u in range(4):
                                t = 4 * t4 + u
                                last = nc.tensor.transpose(
                                    pM[:, u * P:(u + 1) * P],
                                    wint[:, t * TILE_C:t * TILE_C + REG_C, :].rearrange("p x r -> p (x r)"),
                                    ident[:, :])
                            last.then_inc(t_done, 1)
                    t = c - V_AT
                    if on[2] and 0 <= t < NT:
                        n = N - 2
                        gi = next(i for i, tiles in enumerate(VGROUPS) if t in tiles)
                        tiles = VGROUPS[gi]
                        if t == 0:
                            pe.wait_ge(a_done, n * NCH + NCH)
                            pe.wait_ge(xt_done, n * 4 + 4)
                        if t == tiles[0]:
                            wait(pe, (v_act, v_dve)[gi % 2], n * 3 + gi // 2)
                        av = A[q].rearrange("p (k b i x) -> p b k i x", k=TAPS, b=IPG, i=TILE_R)
                        o = (t - tiles[0]) * TAPC
                        for b in range(IPG):
                            last = mm(pV[gi % 2][b * C:(b + 1) * C, o:o + TAPC],
                                      XT[q][:, t * P + b * C:t * P + (b + 1) * C],
                                      av[:, b, :, :, t * TILE_C:(t + 1) * TILE_C], start=True, stop=True)
                        if t == tiles[-1]:
                            last.then_inc(v_done, 1)
                    if on[3] and 0 <= c - CONV_AT < KS:
                        n, kx = N - 3, c - CONV_AT
                        if kx == 0:
                            pe.wait_ge(v2_ld, (n + 1) * (16 * NV2))
                            wait(pe, xt_done, N * 4 if on[1] else PAIRS * 4)
                            wait(pe, out_ready, n)
                            pe.wait_ge(om_act, N + 1 if on[0] else PAIRS)
                        for b in range(IPG):
                            last = mm(pM[b * C:(b + 1) * C, PX:2 * PX], wc[:, kx, :],
                                      v2[:, b, kx, :].rearrange("p (t i j) -> p i t j", t=NT, i=TILE_R),
                                      start=(kx == 0), stop=(kx == KS - 1))
                        if kx == KS - 1:
                            last.then_inc(conv_done, 1)
                    if on[0]:
                        if 0 <= c - OM_AT < KS:
                            kx = c - OM_AT
                            if kx == 0:
                                wait(pe, xt_done, (N - 1) * 4)
                                wait(pe, out_ready, N - 3)
                                pe.wait_ge(wino_ld[q], (N - q) * (8 * KS) + 16 * KS)
                            x0 = LEFT - 1 + kx
                            for b in range(IPG):
                                last = mm(pM[b * C:(b + 1) * C, 0:PX], wom[:, kx, :],
                                          wino[0:KS * C, q, b, :, x0:x0 + W],
                                          start=(kx == 0), stop=(kx == KS - 1))
                            if kx == KS - 1:
                                last.then_inc(om_done, 1)
                        if c in REP_AT:
                            b = REP_AT.index(c)
                            i = N * IPG + b
                            if b == 0:
                                pe.wait_ge(om_split, N + 1)
                            wait(pe, hy_abs, i)
                            wait(pe, hy_full, i)
                            mm(pR[0:STK, 0:PX], seldy_s[:, b, :], om_hi[:, 0, :], start=True, stop=False)
                            mm(pR[0:STK, 0:PX], seldy_s[:, b, :], om_lo[:, 0, :], start=False, stop=True)
                            mm(pR[0:HYR, PX:2 * PX], selm_s[:, b, :], om_hi[:, 1, :], start=True, stop=False)
                            mm(pR[0:HYR, PX:2 * PX], selm_s[:, b, :], om_lo[:, 1, :], start=False,
                               stop=True).then_inc(rep_done, 1)
            steps(pe, step)

            pe.wait_ge(reach_col, 1)
            pe.wait_ge(out_ready, NPAIR * g_count)
            nc.tensor.transpose(pM[0:1, 0:OMG], rmax[:, :], ident[0:OMG, 0:OMG]).then_inc(reach_row, 1)
            pe.wait_ge(flag_set, 1)
            far = pe.value_load(flag_i[0:1, 0:1], min_val=0, max_val=1)
            with pe.If(far > 0):
                pe.wait_ge(g_const, 64)
                for g in range(g_count):
                    with pe.Fori(0, H) as r:
                        pe.wait_ge(g_row_ld, (r + (g * H + 1)) * 16)
                        nc.tensor.transpose(pM[:, 0:P], g_row, ident[:, :]).then_inc(g_row_T, 1)
                for i in range(images):
                    m = g_sem[i // IPG]
                    at0 = (i % IPG) * H
                    with pe.Fori(0, H) as y:
                        pe.wait_ge(m["load"], (y + (at0 + 1)) * 32)
                        for t in range(TAPS):
                            ky, kx = divmod(t, KS)
                            x0 = LEFT - 1 + kx
                            last = mm(pR[:, 0:OMC], g_win[:, ky, x0:x0 + W], g_wom[:, t, :],
                                      start=(t == 0), stop=(t == TAPS - 1))
                        last.then_inc(m["om"], 1)
                        pe.wait_ge(m["own"], (y + (at0 + 1)) * OWN)
                        for j in range(KS):
                            last = nc.tensor.transpose(pM[0:KS * C, j * W:(j + 1) * W],
                                                       g_acc[:, j * KS * C:(j + 1) * KS * C], ident[:, :])
                        last.then_inc(m["valT"], 1)
                        pe.wait_ge(m["copy"], y + (at0 + 1))
                        for j in range(KS):
                            last = mm(pV[0][0:C, 0:W], g_wc[:, j, :], g_vT[:, j * W:(j + 1) * W],
                                      start=(j == 0), stop=(j == KS - 1))
                        last.then_inc(m["conv"], 1)


def constants():
    import numpy as np
    a = {}
    h = np.arange(H)
    f = np.arange(MODES)
    ang = 2 * np.pi * ((h[:, None] * f[None, :]) % H) / H
    a["dft"] = np.concatenate([np.cos(ang), -np.sin(ang)], 1).astype(np.float32)
    wgt = np.where(f == 0, 1.0, 2.0)[:, None] / H
    a["inv"] = np.concatenate([wgt * np.cos(ang.T), -wgt * np.sin(ang.T)], 0).astype(np.float32)
    a["inv"][MODES] = 0.0
    a["ident"] = np.eye(P, dtype=np.float32)
    seldy = np.zeros((OMG, IPG, STK), np.float16)
    selm = np.zeros((OMG, IPG, HYR), np.float16)
    sdx = np.zeros((P, TAPS, P), np.float16)
    shy = np.zeros((P, TAPS, TILE_R, P), np.float16)
    cols = np.zeros((P, 4), np.float32)
    cols[:, 3] = BN_EPS
    for b in range(IPG):
        for k in range(TAPS):
            for q in range(2):
                for s in range(NSH):
                    seldy[b * C + k, b, (q * NSH + s) * TAPS + k] = 1
                    selm[b * C + 2 * TAPS + k, b, (q * NSH + s) * TAPS + k] = 1
                seldy[b * C + TAPS + k, b, DX0 + q * TAPS + k] = 1
            cols[b * C + k, 2] = cols[b * C + TAPS + k, 2] = 3e38
    for q in range(2):
        for s in range(NSH):
            for k in range(TAPS):
                row = (q * NSH + s) * TAPS + k
                cols[row, 0] = REACH - s
                cols[row, 1] = -q
                for i in range(TILE_R):
                    r = i + k // KS + s + TOP - 1 - REACH
                    shy[row, k, i, r::REG_R] = 1
        for k in range(TAPS):
            cols[DX0 + q * TAPS + k, 1] = -q
            sdx[DX0 + q * TAPS + k, k, :] = 1
    col = np.arange(P) // REG_R
    for k in range(TAPS):
        sdx[POSR, k, :] = 1
        sdx[ONER, k, :] = (k % KS) - 1 + LEFT - col
    a["seldy"], a["selm"], a["sdx"], a["shy"], a["cols"] = seldy, selm, sdx, shy, cols
    hsc = np.ones((2, IPG, 2, PX), np.float16)
    hsc[0] = np.arange(PX) % TILE_C
    a["hsconst"] = hsc
    k = np.arange(TAPS)
    a["gtab"] = np.concatenate([np.broadcast_to(k // KS - 1.0, (P, TAPS)),
                                (k % KS - 1.0)[None, :] + np.arange(W)[:, None],
                                np.broadcast_to(np.arange(H) * 1.0, (P, H))], 1).astype(np.float32)
    return a


def kernel(x, L0_conv_w_x_r, L0_conv_w_x_i, L0_conv_w_y_r, L0_conv_w_y_i, L0_conv_mix_w, L0_conv_mix_b,
           L1_conv_w_om, L1_conv_b_om, L1_conv_weight, L1_conv_bias):
    import numpy as np
    import concourse.bacc as bacc
    from concourse.bass_utils import run_bass_kernel_spmd

    order = list(range(0, 2 * TAPS, 2)) + list(range(1, 2 * TAPS, 2)) + list(range(2 * TAPS, 3 * TAPS))
    arrays = {
        "x": x, "wxr": L0_conv_w_x_r, "wxi": L0_conv_w_x_i, "wyr": L0_conv_w_y_r, "wyi": L0_conv_w_y_i,
        "mixt": np.asarray(L0_conv_mix_w).T, "mixb": np.asarray(L0_conv_mix_b).reshape(C, 1),
        "womt": np.asarray(L1_conv_w_om)[order].reshape(OMC, C, TAPS).transpose(2, 1, 0),
        "bom": np.asarray(L1_conv_b_om)[order].reshape(OMC, 1),
        "wct": np.asarray(L1_conv_weight).reshape(C, C, TAPS).transpose(2, 1, 0),
        "biasc": np.asarray(L1_conv_bias).reshape(C, 1),
    }
    arrays.update({k: v for k, v in constants().items()})
    arrays = {k: np.ascontiguousarray(v) for k, v in arrays.items()}
    n = arrays["x"].shape[0]
    nc = bacc.Bacc("TRN2", target_bir_lowering=False, num_devices=1)
    names = ["x", "wxr", "wxi", "wyr", "wyi", "mixt", "mixb", "womt", "bom", "wct", "biasc",
             "dft", "inv", "ident", "seldy", "selm", "sdx", "shy", "hsconst", "cols", "gtab"]
    args = [nc.dram_tensor("in_" + k, arrays[k].shape, mybir.dt.from_np(arrays[k].dtype),
                           kind="ExternalInput").ap() for k in names]
    out = nc.dram_tensor("out", (n * C, HW), fp32, kind="ExternalOutput").ap()
    build(nc, n // IPG, *args, out)
    r = run_bass_kernel_spmd(nc, [{"in_" + k: arrays[k] for k in names}], core_ids=[0])
    return r.results[0]["out"].reshape(n, C, H, W)
```
